# Optimizing a Trainium2 kernel written in Bass

```python
import numpy as np
import jax
import jax.numpy as jnp

def _softmax(x, axis=-1):
    return jax.nn.softmax(x, axis=axis)

def _gelu(x):
    return jax.nn.gelu(x, approximate=True)

def _silu(x):
    return jax.nn.silu(x)

def _sigmoid(x):
    return jax.nn.sigmoid(x)

def _layernorm(x, axis=-1, eps=1e-05):
    m = jnp.mean(x, axis=axis, keepdims=True)
    v = jnp.var(x, axis=axis, keepdims=True)
    return (x - m) / jnp.sqrt(v + eps)

def _scatter_add(tgt, idx, src, axis=0):
    return tgt.at[idx].add(src)

def _segment_sum(src, seg, n):
    return jax.ops.segment_sum(src, seg, n)
kernel_name = 'mk_adj_resnorm_d2_adj_r2_09f9ec'

def setup_inputs(seed: int=0):
    np.random.seed(seed)
    _w = jnp.asarray

    def _rec_inputs():
        import jax
        import jax.numpy as jnp
        _gk = jax.random.key(seed)
        x = 7.22e-05 + 1 * jax.random.normal(jax.random.fold_in(_gk, 1), (128, 128, 512), jnp.float32)
        _a = jax.random.bernoulli(jax.random.fold_in(_gk, 2), 0.0625, (128, 128))
        _a = jnp.logical_or(_a, jnp.swapaxes(_a, -1, -2))
        _a = jnp.logical_or(_a, jnp.eye(128, dtype=bool))
        _af = _a.astype(jnp.float32)
        adj = _af
        return (x, adj)
    x, adj = _rec_inputs()

    def _L0_gnn_setup():
        import jax, jax.numpy as jnp
        import numpy as np
        EPS = 1e-08

        def _row_stochastic_causal(A, causal_mask):
            A = A * causal_mask
            deg = jnp.maximum(A.sum(axis=-1, keepdims=True), EPS)
            return A / deg
        key = jax.random.key(seed)
        k = jax.random.split(key, 5)
        B, N, D = (4, 1024, 512)
        s = 1.0 / np.sqrt(D)
        h = jax.random.normal(k[0], (B, N, D), dtype=jnp.float32)
        W_lang = jax.random.normal(k[1], (D, D), dtype=jnp.float32) * s
        W_grav = jax.random.normal(k[2], (D, D), dtype=jnp.float32) * s
        W_V = jax.random.normal(k[3], (D, D), dtype=jnp.float32) * s
        W_O = jax.random.normal(k[4], (D, D), dtype=jnp.float32) * s
        causal_mask = jnp.tril(jnp.ones((N, N), dtype=jnp.float32))
        gate_logit = jnp.zeros((), jnp.float32)
        log_sigma = jnp.zeros((), jnp.float32)
        return {'h': h, 'causal_mask': causal_mask, 'W_lang': W_lang, 'W_grav': W_grav, 'W_V': W_V, 'W_O': W_O, 'gate_logit': gate_logit, 'log_sigma': log_sigma}
    _L0_gnn_all = _L0_gnn_setup()
    _L0_gnn_in = {k: v for k, v in _L0_gnn_all.items() if k in ('W_lang', 'W_grav', 'W_V', 'W_O', 'gate_logit', 'log_sigma')}
    del _L0_gnn_all

    def _L1_gnn_setup():
        import jax, jax.numpy as jnp
        import numpy as np
        DIM = 199
        K_HOP = 3

        def _khop_support(n, k):
            A = np.eye(n, dtype=np.float64)
            idx = np.arange(n)
            A[idx, (idx + 1) % n] = 1.0
            A[(idx + 1) % n, idx] = 1.0
            S = np.linalg.matrix_power(A, k)
            return (S > 0).astype(np.float32)
        key = jax.random.key(seed)
        kx, kk = jax.random.split(key)
        batch, n, f = (128, DIM, 512)
        x = jax.random.normal(kx, (batch, n, f), dtype=jnp.float32)
        support = jnp.asarray(_khop_support(n, K_HOP))
        limit = float(np.sqrt(6.0 / (n + n)))
        kernel = jax.random.uniform(kk, (n, n), minval=-limit, maxval=limit, dtype=jnp.float32)
        bias = jnp.zeros((f,), dtype=jnp.float32)
        return {'x': x, 'support': support, 'kernel': kernel, 'bias': bias}
    _L1_gnn_all = _L1_gnn_setup()
    _L1_gnn_in = {k: v for k, v in _L1_gnn_all.items() if k in ('bias',)}
    del _L1_gnn_all
    return {'x': x, 'adj': adj, 'L0_gnn_W_lang': _L0_gnn_in['W_lang'], 'L0_gnn_W_grav': _L0_gnn_in['W_grav'], 'L0_gnn_W_V': _L0_gnn_in['W_V'], 'L0_gnn_W_O': _L0_gnn_in['W_O'], 'L0_gnn_gate_logit': _L0_gnn_in['gate_logit'], 'L0_gnn_log_sigma': _L0_gnn_in['log_sigma'], 'L1_gnn_bias': _L1_gnn_in['bias']}

def reference(x, adj, L0_gnn_W_lang, L0_gnn_W_grav, L0_gnn_W_V, L0_gnn_W_O, L0_gnn_gate_logit, L0_gnn_log_sigma, L1_gnn_bias):
    import jax
    import jax.numpy as jnp

    def _L0_gnn_ref(h, causal_mask, W_lang, W_grav, W_V, W_O, gate_logit, log_sigma):
        import jax, jax.numpy as jnp
        import numpy as np
        EPS = 1e-08

        def _row_stochastic_causal(A, causal_mask):
            A = A * causal_mask
            deg = jnp.maximum(A.sum(axis=-1, keepdims=True), EPS)
            return A / deg
        z_l = jnp.einsum('bnd,ed->bne', h, W_lang)
        z_g = jnp.einsum('bnd,ed->bne', h, W_grav)
        v = jnp.einsum('bnd,ed->bne', h, W_V)
        N = h.shape[-2]
        not_eye = 1.0 - jnp.eye(N, dtype=h.dtype)
        zn = z_l / jnp.maximum(jnp.linalg.norm(z_l, axis=-1, keepdims=True), EPS)
        A_l = jnp.maximum(jnp.einsum('bnd,bmd->bnm', zn, zn), 0.0) * not_eye
        sq = jnp.sum(z_g * z_g, axis=-1, keepdims=True)
        d2 = jnp.maximum(sq + jnp.swapaxes(sq, -1, -2) - 2.0 * jnp.einsum('bnd,bmd->bnm', z_g, z_g), 0.0)
        sigma = jnp.exp(log_sigma)
        A_g = jnp.exp(-d2 / (2.0 * sigma * sigma)) * not_eye
        K_l = _row_stochastic_causal(A_l, causal_mask)
        K_g = _row_stochastic_causal(A_g, causal_mask)
        w_l = jax.nn.sigmoid(gate_logit)
        K = w_l * K_l + (1.0 - w_l) * K_g
        out = jnp.einsum('bnm,bmd->bnd', K, v)
        return jnp.einsum('bnd,ed->bne', out, W_O)

    def _L1_gnn_ref(x, support, kernel, bias):
        import jax, jax.numpy as jnp
        import numpy as np
        DIM = 199
        K_HOP = 3

        def _khop_support(n, k):
            A = np.eye(n, dtype=np.float64)
            idx = np.arange(n)
            A[idx, (idx + 1) % n] = 1.0
            A[(idx + 1) % n, idx] = 1.0
            S = np.linalg.matrix_power(A, k)
            return (S > 0).astype(np.float32)
        W = support * kernel
        out = jnp.einsum('bnf,nm->bmf', x, W)
        out = out + bias
        return out
    x = _layernorm(x + _L0_gnn_ref(x, adj, L0_gnn_W_lang, L0_gnn_W_grav, L0_gnn_W_V, L0_gnn_W_O, L0_gnn_gate_logit, L0_gnn_log_sigma), axis=-1)
    x = _layernorm(x + _L1_gnn_ref(x, adj, adj, L1_gnn_bias), axis=-1)
    return x

_drawn_inputs = setup_inputs


def setup_inputs(seed=0):
    import zlib

    import numpy as np

    out = dict(_drawn_inputs(seed))
    spreads = {'L1_gnn_bias': (0.0, 0.34)}
    factors = {}
    for name, (base, spread) in spreads.items():
        noise = np.random.default_rng([zlib.crc32(name.encode()), seed]).standard_normal(out[name].shape)
        drawn = base * np.exp(spread * noise) if base else spread * noise
        out[name] = jnp.asarray(drawn.astype(out[name].dtype))
    for name, factor in factors.items():
        out[name] = (out[name] * factor).astype(out[name].dtype)
    return out
```

```python
from contextlib import ExitStack

import concourse.bass as bass
from concourse import mybir

ALU = mybir.AluOpType
ACT = mybir.ActivationFunctionType
F32 = mybir.dt.float32
F32R = mybir.dt.float32r

P = 128
GROUP = 4
EPS = 1e-8
LN_EPS = 1e-5


def build(nc, xt_d, x_d, adj_d, wlang_d, wgrav_d, wv_d, wot_d, gate_d, sigma_d, bias_d, out_d):
    B, N, D = x_d.shape
    C = D // P
    GROUPS = B // GROUP
    LOOPS = (GROUPS - 4) // 2
    PAIR = 2 * GROUP
    assert N == P and C == GROUP and GROUPS % 2 == 0 and LOOPS >= 1

    row_at = [sum(C - k for k in range(d)) for d in range(C)]
    BLOCKS = sum(C - k for k in range(C))

    with ExitStack() as ctx:
        def sb(name, shape, dt=F32):
            return ctx.enter_context(nc.sbuf_tensor(name, shape, dt))

        def bank(name):
            return ctx.enter_context(nc.psum_tensor(name, [P, 512], F32))

        def sem(name):
            return ctx.enter_context(nc.semaphore(name))

        u_w = sb("u_w", [P, 2, 2, BLOCKS, P], F32R)
        vo_w = sb("vo_w", [P, 2, C, D], F32R)
        xt = sb("xt", [P, 2, C, GROUP * P])
        xn = sb("xn", [P, 2, GROUP, D])
        ht = sb("ht", [P, 2, 2, C, GROUP, P], F32R)
        hu = sb("hu", [P, 2, 2, C, GROUP, 2, P], F32R)
        v = sb("v", [P, 2, 2, D], F32R)
        x1 = sb("x1", [P, 2, 2, D], F32R)
        kt = sb("kt", [P, 2, 2, P], F32R)
        w1 = sb("w1", [P, 2, P], F32R)
        p_sb = sb("p_sb", [P, 2, 2 * P])
        scores = sb("scores", [P, 2 * P])
        near = sb("near", [P, P])
        gauss = sb("gauss", [P, P])
        edges = sb("edges", [P, 2, 2, P])
        kmix = sb("kmix", [P, P])
        kmat = sb("kmat", [P, P])
        res1 = sb("res1", [P, D])
        x1f = sb("x1f", [P, D])
        res2 = sb("res2", [P, 2, D])
        y = sb("y", [P, 2, D])
        half_sq = sb("half_sq", [P, 2, 2])
        sq_floor = sb("sq_floor", [P, 2])
        inv_norm = sb("inv_norm", [P, 2])
        exp_bias = sb("exp_bias", [P, 2])
        degree = sb("degree", [P, 2, 2])
        floored = sb("floored", [P, 2, 2])
        recip = sb("recip", [P, 2, 2])
        share = sb("share", [P, 2, 2])
        coef = sb("coef", [P, 2, 2])
        stats = sb("stats", [P, 2, 6])
        moments = sb("moments", [P, 2, 2, 2])
        var_eps = sb("var_eps", [P, 2, 2])
        rstd = sb("rstd", [P, 2, 2])
        shift = sb("shift", [P, 2])
        ident = sb("ident", [P, P])
        adj = sb("adj", [P, P])
        mask = sb("mask", [P, P])
        w1f = sb("w1f", [P, 2, P])
        bias = sb("bias", [P, D])
        powers = sb("powers", [P, 2, 2])
        gates = sb("gates", [P, 8])
        gate, log_sigma, e_gate, sigma, one_e, w_l, inv_s2, neg_inv_s2 = (gates[:, k:k + 1] for k in range(8))
        sig_sq = sb("sig_sq", [P, 1])

        v_ps, hul_ps, hug_ps = bank("v_ps"), bank("hul_ps"), bank("hug_ps")
        s_ps = [bank("s0_ps"), bank("s1_ps")]
        kv_ps, l1_ps, setup_ps = bank("kv_ps"), bank("l1_ps"), bank("setup_ps")

        w_in = [sem(f"w_in{k}") for k in range(4)]
        adj_in, small_in = sem("adj_in"), sem("small_in")
        xt_in = [sem("xt_in0"), sem("xt_in1")]
        xn_in = [sem("xn_in0"), sem("xn_in1")]
        stored = [sem("stored0"), sem("stored1")]
        ident_set, consts_set, mask_set = sem("ident_set"), sem("consts_set"), sem("mask_set")
        w_hi, w_lo = sem("w_hi"), sem("w_lo")
        products = sem("products")
        prod_hi, prod_lo = sem("prod_hi"), sem("prod_lo")
        gate_exp, gate_ops = sem("gate_exp"), sem("gate_ops")
        w1_sum, w1_hi, w1_lo = sem("w1_sum"), sem("w1_hi"), sem("w1_lo")
        ht_hi, ht_lo = sem("ht_hi"), sem("ht_lo")
        hul_mm, hul_hi, hul_lo = sem("hul_mm"), sem("hul_hi"), sem("hul_lo")
        hug_mm, hug_hi, hug_lo = sem("hug_mm"), sem("hug_hi"), sem("hug_lo")
        v_mm, v_hi, v_lo = sem("v_mm"), sem("v_hi"), sem("v_lo")
        p_mm, p_out, diag = sem("p_mm"), sem("p_out"), sem("diag")
        floor_set, norm_set, bias_set, share_set = sem("floor_set"), sem("norm_set"), sem("bias_set"), sem("share_set")
        turned = sem("turned")
        scores_set, near_set, gauss_arg, gauss_exp = sem("scores_set"), sem("near_set"), sem("gauss_arg"), sem("gauss_exp")
        edges_l, edges_g = sem("edges_l"), sem("edges_g")
        deg_floor, deg_recip, coef_set = sem("deg_floor"), sem("deg_recip"), sem("coef_set")
        mix_l, k_set = sem("mix_l"), sem("k_set")
        kt_mm, kt_hi, kt_lo = sem("kt_mm"), sem("kt_hi"), sem("kt_lo")
        kv_mm, res1_set, stats1, moments1 = sem("kv_mm"), sem("res1_set"), sem("stats1"), sem("moments1")
        x1_set, x1_hi, x1_lo = sem("x1_set"), sem("x1_hi"), sem("x1_lo")
        l1_mm, res2_set, stats2, moments2 = sem("l1_mm"), sem("res2_set"), sem("stats2"), sem("moments2")
        var_set, rstd_set, shift_set, y_set = sem("var_set"), sem("rstd_set"), sem("shift_set"), sem("y_set")

        xt_groups = xt_d
        xn_groups = x_d.rearrange("(g b) n d -> g n b d", b=GROUP)

        w_raw = [xt[:, 0], xt[:, 1], xn[:, 0], xn[:, 1]]
        w_dram = [wlang_d, wgrav_d, wv_d, wot_d]
        hu_flat = [hu[:, k].rearrange("p g c b l n -> p (g c b l n)") for k in range(2)]

        def w_split(part, k, e):
            at = (k * C + e) * D
            return hu_flat[part][:, at:at + D]

        set_a = [kv_ps, l1_ps, s_ps[0], s_ps[1]]
        set_b = [v_ps, hul_ps, hug_ps, setup_ps]
        PRODUCTS = [(0, 0, set_a, "l"), (1, 1, set_b, "g"), (2, 3, set_a, "vo")]

        def product_row(n, d):
            left, right, banks, kind = PRODUCTS[n]
            if kind == "vo":
                return banks[d][:, :], [vo_w[:, part, d, :] for part in range(2)], D
            width = (C - d) * P
            parts = [u_w[:, part, n, row_at[d]:row_at[d] + C - d, :].rearrange("p k n -> p (k n)")
                     for part in range(2)]
            return banks[d][:, 0:width], parts, width

        def raw_chunk(m):
            g, c = (m // C) % 2, m % C
            return xt[:, g, c, :], [ht[:, part, g, c, :, :].rearrange("p b n -> p (b n)") for part in range(2)]

        def hu_chunk(part, m, kind):
            return hu[:, part, (m // C) % 2, m % C, :, kind, :]

        def by_graph(ap):
            return ap.rearrange("p (b n) -> p b n", n=P)

        PASSES = ((0, 0), (0, 1), (1, 0))

        def run(eng, slot):
            counts = range(B + 2 * C)
            for m in range(GROUP):
                slot(m, 0, counts)
            with eng.Fori(0, LOOPS) as t:
                n = {k: eng.snap(eng.to_reg(k + PAIR * t), min_val=k, max_val=k + PAIR * (LOOPS - 1)) for k in range(GROUP - 2, GROUP + PAIR + 6)}
                for m in range(GROUP, GROUP + PAIR):
                    slot(m, t, n)
            for m in range(GROUP + PAIR * LOOPS, B + 2):
                slot(m, 0, counts)

        block = ctx.enter_context(nc.Block())

        @block.sync
        def _(sp):
            for k in range(4):
                sp.dma_start(w_raw[k], w_dram[k].rearrange("(e p) d -> p e d", p=P)).then_inc(w_in[k], 16)
            sp.wait_ge(w_lo, C)
            sp.dma_start(xt[:, 0], xt_groups[0]).then_inc(xt_in[0], 16)
            sp.wait_ge(w_lo, 2 * C)
            sp.dma_start(xt[:, 1], xt_groups[1]).then_inc(xt_in[1], 16)
            sp.wait_ge(w_lo, 3 * C)
            sp.dma_start(xn[:, 0], xn_groups[0]).then_inc(xn_in[0], 16)
            sp.wait_ge(w_lo, 4 * C)
            sp.dma_start(xn[:, 1], xn_groups[1]).then_inc(xn_in[1], 16)

            def slot(m, t, n):
                if m == 0:
                    sp.wait_ge(ht_lo, C)
                    sp.dma_start(xt[:, 0], xt_groups[2]).then_inc(xt_in[0], 16)
                group = (m + 5) // C + 2
                if m % C == 2 and group < GROUPS:
                    sp.wait_ge(ht_lo, n[m + 6])
                    sp.dma_start(xt[:, group % 2], xt_groups[group + 2 * t]).then_inc(xt_in[group % 2], 16)
                group = m // C + 1
                if m % C == 0 and 2 <= group < GROUPS:
                    sp.wait_ge(res1_set, n[m])
                    sp.dma_start(xn[:, group % 2], xn_groups[group + 2 * t]).then_inc(xn_in[group % 2], 16)
                if m >= 2:
                    sp.wait_ge(y_set, n[m - 1])
                    sp.dma_start(out_d[m - 2 + PAIR * t], y[:, m % 2, :]).then_inc(stored[m % 2], 16)

            run(sp, slot)
            for k in range(2):
                sp.wait_ge(stored[k], 16 * (B // 2))

        @block.tensor
        def _(pe):
            for n, (left, right, banks, kind) in enumerate(PRODUCTS):
                if n == 2:
                    pe.wait_ge(prod_lo, C)
                for e in range(C):
                    pe.wait_ge(w_lo, right * C + e + 1)
                    for d in range(C):
                        out, _, width = product_row(n, d)
                        for a, b in PASSES:
                            mm = pe.matmul(out, w_split(a, left, e)[:, d * P:(d + 1) * P],
                                           w_split(b, right, e)[:, D - width:D],
                                           start=(e == 0 and (a, b) == PASSES[0]),
                                           stop=(e == C - 1 and (a, b) == PASSES[-1]))
                mm.then_inc(products, 1)

            def project(bank_ps, kind, m):
                d_out = m % C
                _, (hi, lo) = raw_chunk(m)
                for d in range(d_out + 1):
                    _, moving = raw_chunk(m - d_out + d)
                    for a, b in PASSES:
                        mm = pe.matmul(bank_ps[:, :], u_w[:, a, kind, row_at[d] + d_out - d, :], moving[b],
                                       start=(d == 0 and (a, b) == PASSES[0]),
                                       stop=(d == d_out and (a, b) == PASSES[-1]))
                return mm

            def values(m):
                for c in range(C):
                    for a, b in PASSES:
                        mm = pe.matmul(v_ps[:, :], ht[:, a, (m // GROUP) % 2, c, m % GROUP, :], vo_w[:, b, c, :],
                                       start=(c == 0 and (a, b) == PASSES[0]),
                                       stop=(c == C - 1 and (a, b) == PASSES[-1]))
                return mm

            for m in range(C):
                pe.wait_ge(ht_lo, m + 1)
                if m == 0:
                    pe.wait_ge(prod_lo, 2 * C)
                else:
                    pe.wait_ge(hul_lo, m)
                project(hul_ps, 0, m).then_inc(hul_mm, 1)
                if m > 0:
                    pe.wait_ge(hug_lo, m)
                project(hug_ps, 1, m).then_inc(hug_mm, 1)
            pe.wait_ge(prod_lo, 3 * C)
            values(0).then_inc(v_mm, 1)
            pe.wait_ge(ident_set, 3)
            pe.wait_ge(w1_lo, 1)

            def slot(m, t, n):
                s = s_ps[m % 2]
                if m < B:
                    if m % GROUP == 0:
                        pe.wait_ge(hul_lo, n[m + GROUP])
                        pe.wait_ge(hug_lo, n[m + GROUP])
                    for c in range(C):
                        for a, b in PASSES:
                            mm = pe.matmul(s[:, 0:2 * P], ht[:, a, (m // GROUP) % 2, c, m % GROUP, :],
                                           hu[:, b, (m // GROUP) % 2, c, m % GROUP, :, :],
                                           start=(c == 0 and (a, b) == PASSES[0]),
                                           stop=(c == C - 1 and (a, b) == PASSES[-1]))
                    mm.then_inc(p_mm, 1)
                if m >= 2:
                    pe.wait_ge(x1_lo, n[m - 1])
                    if m >= 3:
                        pe.wait_ge(res2_set, n[m - 2])
                    for a, b in PASSES:
                        mm = pe.matmul(l1_ps[:, :], w1[:, a, :], x1[:, b, m % 2, :],
                                       start=(a, b) == PASSES[0], stop=(a, b) == PASSES[-1])
                    mm.then_inc(l1_mm, 1)
                if 1 <= m <= B:
                    pe.wait_ge(k_set, n[m])
                    pe.transpose(s_ps[(m - 1) % 2][:, 0:P], kmat[:, :], ident[:, :]).then_inc(kt_mm, 1)
                if m < B - GROUP:
                    pe.wait_ge(ht_lo, n[m + 5])
                    pe.wait_ge(hul_lo, n[m + 4])
                    project(hul_ps, 0, m + C).then_inc(hul_mm, 1)
                if 1 <= m <= B:
                    pe.wait_ge(kt_lo, n[m])
                    pe.wait_ge(v_lo, n[m])
                    if m >= 2:
                        pe.wait_ge(res1_set, n[m - 1])
                    for a, b in PASSES:
                        mm = pe.matmul(kv_ps[:, :], kt[:, a, (m - 1) % 2, :], v[:, b, (m - 1) % 2, :],
                                       start=(a, b) == PASSES[0], stop=(a, b) == PASSES[-1])
                    mm.then_inc(kv_mm, 1)
                if m < B - GROUP:
                    pe.wait_ge(hug_lo, n[m + 4])
                    project(hug_ps, 1, m + C).then_inc(hug_mm, 1)
                if m < B:
                    pe.wait_ge(p_out, n[m + 1])
                    pe.transpose(s[:, 0:P], p_sb[:, m % 2, 0:P], ident[:, :])
                    pe.transpose(s[:, P:2 * P], p_sb[:, m % 2, P:2 * P], ident[:, :])
                    pe.wait_ge(diag, n[m + 1])
                    pe.transpose(s[:, 3 * P:4 * P], half_sq[:, m % 2, 1:2].broadcast_to([P, P]), ident[:, :])
                    pe.wait_ge(norm_set, n[m + 1])
                    pe.transpose(s[:, 2 * P:3 * P], inv_norm[:, m % 2:m % 2 + 1].broadcast_to([P, P]),
                                 ident[:, :]).then_inc(turned, 1)
                if m + 1 < B:
                    pe.wait_ge(v_lo, n[m + 1])
                    values(m + 1).then_inc(v_mm, 1)

            run(pe, slot)

        @block.scalar
        def _(act):
            act.dma_start(adj[:, :], adj_d).then_inc(adj_in, 16)
            act.dma_start(gate, gate_d.partition_broadcast(P)).then_inc(small_in, 16)
            act.dma_start(log_sigma, sigma_d.partition_broadcast(P)).then_inc(small_in, 16)
            act.dma_start(bias[:, :], bias_d.partition_broadcast(P)).then_inc(small_in, 16)

            def split_weight(k):
                for e in range(C):
                    if e == 0:
                        act.wait_ge(w_in[k], 16)
                    act.activation(w_split(0, k, e), w_raw[k][:, e, :], ACT.Copy).then_inc(w_hi, 1)

            def split_product(n):
                act.wait_ge(products, n + 1)
                for d in range(C):
                    ps, (hi, _), width = product_row(n, d)
                    if n < 2:
                        act.activation(hi[:, 0:P], ps[:, 0:P], ACT.Copy, scale=0.5)
                        if width > P:
                            act.activation(hi[:, P:width], ps[:, P:width], ACT.Copy)
                    else:
                        act.activation(hi, ps, ACT.Copy)
                    act.drain().then_inc(prod_hi, 1)

            def split_ht(m):
                raw, (hi, _) = raw_chunk(m)
                act.activation(hi, raw, ACT.Copy).then_inc(ht_hi, 1)

            split_weight(0)
            split_weight(1)
            split_product(0)
            split_weight(2)
            split_weight(3)
            act.wait_ge(small_in, 48)
            act.activation(e_gate, gate, ACT.Exp, scale=-1.0).then_inc(gate_exp, 1)
            act.activation(sigma, log_sigma, ACT.Exp).then_inc(gate_exp, 1)
            act.wait_ge(w1_sum, 2)
            act.activation(w1[:, 0, :], w1f[:, 1, :], ACT.Copy).then_inc(w1_hi, 1)
            act.wait_ge(xt_in[0], 16)
            for m in range(C):
                split_ht(m)
            split_product(1)
            act.wait_ge(xt_in[1], 16)
            split_ht(C)
            split_product(2)
            for m in range(C):
                act.wait_ge(hul_mm, m + 1)
                act.activation(hu_chunk(0, m, 0), by_graph(hul_ps[:, :]), ACT.Copy).then_inc(hul_hi, 1)
                act.wait_ge(hug_mm, m + 1)
                act.activation(hu_chunk(0, m, 1), by_graph(hug_ps[:, :]), ACT.Copy).then_inc(hug_hi, 1)

            def slot(m, t, n):
                if m < B:
                    act.wait_ge(v_mm, n[m + 1])
                    act.activation(v[:, 0, m % 2, :], v_ps[:, :], ACT.Copy).then_inc(v_hi, 1)
                    act.wait_ge(p_mm, n[m + 1])
                    act.activation(p_sb[:, m % 2, :], s_ps[m % 2][:, 0:2 * P], ACT.Copy).then_inc(p_out, 1)
                if 1 <= m <= B:
                    act.wait_ge(kt_mm, n[m])
                    act.activation(kt[:, 0, (m - 1) % 2, :], s_ps[(m - 1) % 2][:, 0:P], ACT.Copy).then_inc(kt_hi, 1)
                if m + 5 < B:
                    if (m + 5) % C == 0:
                        group = (m + 5) // C
                        act.wait_ge(xt_in[group % 2], 16 * (group // 2 + 1) + 16 * t)
                    split_ht(m + 5)
                if m < B - GROUP:
                    act.wait_ge(hul_mm, n[m + 5])
                    act.activation(hu_chunk(0, m + C, 0), by_graph(hul_ps[:, :]), ACT.Copy).then_inc(hul_hi, 1)
                    act.wait_ge(hug_mm, n[m + 5])
                    act.activation(hu_chunk(0, m + C, 1), by_graph(hug_ps[:, :]), ACT.Copy).then_inc(hug_hi, 1)
                if m >= 2:
                    act.wait_ge(shift_set, n[m - 1])
                    if m >= 4:
                        act.wait_ge(stored[m % 2], 16 * (m // 2 - 1) + 16 * GROUP * t)
                    act.activation(y[:, m % 2, :], res2[:, m % 2, :], ACT.Identity, scale=rstd[:, m % 2, 1:2],
                                   bias=shift[:, m % 2:m % 2 + 1]).then_inc(y_set, 1)
                if m < B:
                    act.wait_ge(gauss_arg, n[m + 1])
                    act.wait_ge(bias_set, n[m + 1])
                    act.activation(gauss[:, :], near[:, :], ACT.Exp, scale=inv_s2,
                                   bias=exp_bias[:, m % 2:m % 2 + 1]).then_inc(gauss_exp, 1)
                if 1 <= m <= B:
                    act.wait_ge(x1_set, n[m])
                    act.activation(x1[:, 0, (m - 1) % 2, :], x1f[:, :], ACT.Copy).then_inc(x1_hi, 1)

            run(act, slot)

        @block.vector
        def _(dve):
            def rest(out, full, hi):
                return dve.tensor_tensor(out, full, hi.bitcast(F32), ALU.subtract)

            def split_weight(k):
                for e in range(C):
                    dve.wait_ge(w_hi, k * C + e + 1)
                    rest(w_split(1, k, e), w_raw[k][:, e, :], w_split(0, k, e)).then_inc(w_lo, 1)

            def split_product(n):
                for d in range(C):
                    dve.wait_ge(prod_hi, n * C + d + 1)
                    ps, (hi, lo), width = product_row(n, d)
                    if n < 2:
                        last = dve.scalar_tensor_tensor(lo[:, 0:P], ps[:, 0:P], 0.5, hi[:, 0:P].bitcast(F32),
                                                        ALU.mult, ALU.subtract)
                        if width > P:
                            last = rest(lo[:, P:width], ps[:, P:width], hi[:, P:width])
                    else:
                        last = rest(lo, ps, hi)
                    last.then_inc(prod_lo, 1)

            dve.wait_ge(adj_in, 16)
            dve.tensor_tensor(w1f[:, 0, :], adj[:, :], adj[:, :], ALU.mult).then_inc(w1_sum, 1)
            dve.wait_ge(w1_sum, 1)
            dve.wait_ge(ident_set, 3)
            dve.tensor_tensor(w1f[:, 1, :], w1f[:, 0, :], ident[:, :], ALU.add).then_inc(w1_sum, 1)
            split_weight(0)
            split_weight(1)
            split_product(0)
            split_weight(2)
            split_weight(3)
            dve.wait_ge(w1_hi, 1)
            rest(w1[:, 1, :], w1f[:, 1, :], w1[:, 0, :]).then_inc(w1_lo, 1)
            dve.wait_ge(gate_exp, 2)
            dve.tensor_scalar(one_e, e_gate, 1.0, None, ALU.add).then_inc(gate_ops, 1)
            dve.tensor_tensor(sig_sq[:, :], sigma, sigma, ALU.mult).then_inc(gate_ops, 1)
            dve.wait_ge(gate_ops, 2)
            dve.reciprocal(w_l, one_e).then_inc(gate_ops, 1)
            dve.reciprocal(inv_s2, sig_sq[:, :]).then_inc(gate_ops, 1)
            dve.wait_ge(gate_ops, 4)
            dve.tensor_scalar(neg_inv_s2, inv_s2, -1.0, None, ALU.mult).then_inc(gate_ops, 1)
            for k in range(2):
                dve.tensor_scalar(share[:, k, 1:2], w_l, -1.0, 1.0, ALU.mult, ALU.add).then_inc(gate_ops, 1)
            split_product(1)
            split_product(2)
            for m in range(C):
                dve.wait_ge(hul_hi, m + 1)
                rest(hu_chunk(1, m, 0), by_graph(hul_ps[:, :]), hu_chunk(0, m, 0)).then_inc(hul_lo, 1)
                dve.wait_ge(hug_hi, m + 1)
                rest(hu_chunk(1, m, 1), by_graph(hug_ps[:, :]), hu_chunk(0, m, 1)).then_inc(hug_lo, 1)
            dve.wait_ge(mask_set, 1)

            def slot(m, t, n):
                q = (m - 1) % 2
                s = s_ps[m % 2]
                if m < B:
                    dve.wait_ge(v_hi, n[m + 1])
                    rest(v[:, 1, m % 2, :], v_ps[:, :], v[:, 0, m % 2, :]).then_inc(v_lo, 1)
                if 1 <= m <= B:
                    dve.wait_ge(coef_set, n[m])
                    dve.tensor_scalar(kmix[:, :], edges[:, q, 0, :], coef[:, q, 0:1], None, ALU.mult).then_inc(mix_l, 1)
                if m < B:
                    dve.wait_ge(p_out, n[m + 1])
                    dve.tensor_tensor_reduce(scores[:, 0:P], p_sb[:, m % 2, 0:P], ident[:, :], 1.0, 0.0,
                                             ALU.mult, ALU.add, half_sq[:, m % 2, 0:1])
                if 1 <= m <= B:
                    dve.wait_ge(mix_l, n[m])
                    dve.scalar_tensor_tensor(kmat[:, :], edges[:, q, 1, :], coef[:, q, 1:2], kmix[:, :],
                                             ALU.mult, ALU.add).then_inc(k_set, 1)
                if m < B:
                    dve.tensor_tensor_reduce(scores[:, P:2 * P], p_sb[:, m % 2, P:2 * P], ident[:, :], 1.0, 0.0,
                                             ALU.mult, ALU.add, half_sq[:, m % 2, 1:2]).then_inc(diag, 1)
                if m >= 2:
                    dve.wait_ge(l1_mm, n[m - 1])
                    dve.tensor_tensor(res2[:, m % 2, :], l1_ps[:, :], bias[:, :], ALU.add).then_inc(res2_set, 1)
                if 1 <= m <= B:
                    dve.wait_ge(kt_hi, n[m])
                    rest(kt[:, 1, q, :], s_ps[q][:, 0:P], kt[:, 0, q, :]).then_inc(kt_lo, 1)
                if m >= 2:
                    dve.wait_ge(res2_set, n[m - 1])
                    dve.bn_stats(stats[:, 1, :], res2[:, m % 2, :]).then_inc(stats2, 1)
                if m < B - GROUP:
                    dve.wait_ge(hul_hi, n[m + 5])
                    rest(hu_chunk(1, m + C, 0), by_graph(hul_ps[:, :]), hu_chunk(0, m + C, 0)).then_inc(hul_lo, 1)
                if m >= 2:
                    dve.wait_ge(ident_set, 1)
                    dve.wait_ge(stats2, n[m - 1])
                    dve.bn_aggr(moments[:, m % 2, 1, :], stats[:, 1, :]).then_inc(moments2, 1)
                if 1 <= m <= B:
                    dve.wait_ge(kv_mm, n[m])
                    if (m - 1) % GROUP == 0:
                        group = (m - 1) // GROUP
                        dve.wait_ge(xn_in[group % 2], 16 * (group // 2 + 1) + 16 * t)
                    dve.tensor_tensor(res1[:, :], kv_ps[:, :], xn[:, ((m - 1) // GROUP) % 2, (m - 1) % GROUP, :],
                                      ALU.add).then_inc(res1_set, 1)
                    dve.wait_ge(res1_set, n[m])
                    dve.bn_stats(stats[:, 0, :], res1[:, :]).then_inc(stats1, 1)
                    dve.wait_ge(ident_set, 1)
                    dve.wait_ge(stats1, n[m])
                    dve.bn_aggr(moments[:, m % 2, 0, :], stats[:, 0, :]).then_inc(moments1, 1)
                if m < B - GROUP:
                    dve.wait_ge(hug_hi, n[m + 5])
                    rest(hu_chunk(1, m + C, 1), by_graph(hug_ps[:, :]), hu_chunk(0, m + C, 1)).then_inc(hug_lo, 1)
                if m < B:
                    dve.wait_ge(turned, n[m + 1])
                    dve.wait_ge(diag, n[m + 1])
                    dve.tensor_tensor(scores[:, :], s[:, 0:2 * P], p_sb[:, m % 2, :], ALU.add).then_inc(scores_set, 1)
                    dve.tensor_tensor(edges[:, m % 2, 1, :], s[:, 2 * P:3 * P], mask[:, :], ALU.mult).then_inc(near_set, 1)
                    dve.wait_ge(scores_set, n[m + 1])
                    dve.tensor_tensor(near[:, :], scores[:, P:2 * P], s[:, 3 * P:4 * P], ALU.subtract).then_inc(gauss_arg, 1)
                    dve.wait_ge(near_set, n[m + 1])
                    dve.scalar_tensor_tensor(edges[:, m % 2, 0, :], scores[:, 0:P], 0.0, edges[:, m % 2, 1, :],
                                             ALU.max, ALU.mult, accum_out=degree[:, m % 2, 0:1]).then_inc(edges_l, 1)
                if 1 <= m <= B:
                    dve.wait_ge(rstd_set, n[m])
                    dve.tensor_scalar(x1f[:, :], res1[:, :], moments[:, m % 2, 0, 0:1], rstd[:, m % 2, 0:1],
                                      ALU.subtract, ALU.mult).then_inc(x1_set, 1)
                if m < B:
                    dve.wait_ge(gauss_exp, n[m + 1])
                    dve.wait_ge(edges_l, n[m + 1])
                    dve.scalar_tensor_tensor(edges[:, m % 2, 1, :], gauss[:, :], 1.0, mask[:, :],
                                             ALU.min, ALU.mult, accum_out=degree[:, m % 2, 1:2]).then_inc(edges_g, 1)
                if 1 <= m <= B:
                    dve.wait_ge(x1_hi, n[m])
                    rest(x1[:, 1, q, :], x1f[:, :], x1[:, 0, q, :]).then_inc(x1_lo, 1)

            run(dve, slot)

        @block.gpsimd
        def _(pool):
            pool.memset(ident[:, :], 0.0).then_inc(ident_set, 1)
            pool.memset(powers[:, 0, :], -0.5).then_inc(consts_set, 1)
            pool.memset(powers[:, 1, :], -1.0).then_inc(consts_set, 1)
            pool.wait_ge(ident_set, 1)
            pool.affine_select(out=ident[:, :], in_=ident[:, :], compare_op=ALU.not_equal, fill=1.0, base=0,
                               pattern=[[-1, P]], channel_multiplier=1).then_inc(ident_set, 2)
            pool.wait_ge(adj_in, 16)
            pool.affine_select(out=mask[:, :], in_=adj[:, :], compare_op=ALU.not_equal, fill=0.0, base=0,
                               pattern=[[-1, P]], channel_multiplier=1).then_inc(mask_set, 1)

            def split_ht(m):
                raw, (hi, lo) = raw_chunk(m)
                pool.tensor_tensor(lo, raw, hi.bitcast(F32), ALU.subtract).then_inc(ht_lo, 1)

            for m in range(C + 1):
                pool.wait_ge(ht_hi, m + 1)
                split_ht(m)
            pool.wait_ge(consts_set, 2)
            pool.wait_ge(gate_ops, 7)

            def slot(m, t, n):
                p = m % 2
                if m < B:
                    pool.wait_ge(ident_set, 1)
                    pool.wait_ge(diag, n[m + 1])
                    pool.tensor_scalar(sq_floor[:, p:p + 1], half_sq[:, p, 0:1], 2.0, EPS * EPS,
                                       ALU.mult, ALU.max).then_inc(floor_set, 1)
                    pool.wait_ge(floor_set, n[m + 1])
                    pool.tensor_tensor(inv_norm[:, p:p + 1], sq_floor[:, p:p + 1], powers[:, 0, 0:1],
                                       ALU.pow).then_inc(norm_set, 1)
                    pool.tensor_scalar(exp_bias[:, p:p + 1], half_sq[:, p, 1:2], neg_inv_s2, None,
                                       ALU.mult).then_inc(bias_set, 1)
                    pool.wait_ge(ident_set, 1)
                    pool.wait_ge(norm_set, n[m + 1])
                    pool.tensor_scalar(share[:, p, 0:1], inv_norm[:, p:p + 1], w_l, None, ALU.mult).then_inc(share_set, 1)
                if m + 5 < B:
                    pool.wait_ge(ht_hi, n[m + 6])
                    split_ht(m + 5)
                if m >= 1:
                    a, b = (0 if m <= B else 1), (2 if m >= 2 else 1)
                    pool.wait_ge(ident_set, 1)
                    if m <= B:
                        pool.wait_ge(moments1, n[m])
                    if m >= 2:
                        pool.wait_ge(moments2, n[m - 1])
                    pool.tensor_scalar(var_eps[:, p, a:b], moments[:, p, a:b, 1], LN_EPS, None, ALU.add).then_inc(var_set, 1)
                    pool.wait_ge(var_set, n[m])
                    pool.tensor_tensor(rstd[:, p, a:b], var_eps[:, p, a:b], powers[:, 0, a:b], ALU.pow).then_inc(rstd_set, 1)
                if m >= 2:
                    pool.wait_ge(ident_set, 1)
                    pool.wait_ge(rstd_set, n[m])
                    pool.tensor_scalar(shift[:, p:p + 1], moments[:, p, 1, 0:1], -1.0, rstd[:, p, 1:2],
                                       ALU.mult, ALU.mult).then_inc(shift_set, 1)
                if m < B:
                    pool.wait_ge(ident_set, 1)
                    pool.wait_ge(edges_l, n[m + 1])
                    pool.tensor_scalar(floored[:, p, 0:1], degree[:, p, 0:1], inv_norm[:, p:p + 1], EPS,
                                       ALU.mult, ALU.max)
                    pool.wait_ge(ident_set, 1)
                    pool.wait_ge(edges_g, n[m + 1])
                    pool.tensor_scalar(floored[:, p, 1:2], degree[:, p, 1:2], EPS, None, ALU.max).then_inc(deg_floor, 1)
                    pool.wait_ge(deg_floor, n[m + 1])
                    pool.tensor_tensor(recip[:, p, :], floored[:, p, :], powers[:, 1, :], ALU.pow).then_inc(deg_recip, 1)
                    pool.wait_ge(deg_recip, n[m + 1])
                    pool.wait_ge(share_set, n[m + 1])
                    pool.tensor_tensor(coef[:, p, :], recip[:, p, :], share[:, p, :], ALU.mult).then_inc(coef_set, 1)

            run(pool, slot)


def kernel(x, adj, L0_gnn_W_lang, L0_gnn_W_grav, L0_gnn_W_V, L0_gnn_W_O, L0_gnn_gate_logit, L0_gnn_log_sigma,
           L1_gnn_bias):
    import numpy as np
    import concourse.bacc as bacc
    from concourse.bass_utils import run_bass_kernel_spmd

    x = np.asarray(x)
    batch, nodes, dim = x.shape
    xt = x.reshape(batch // GROUP, GROUP, nodes, dim // P, P).transpose(0, 4, 3, 1, 2)
    arrays = {
        "xt_dram": np.ascontiguousarray(xt).reshape(batch // GROUP, P, dim // P, GROUP * nodes),
        "x_dram": np.ascontiguousarray(x),
        "adj_dram": np.ascontiguousarray(adj),
        "w_lang_dram": np.ascontiguousarray(L0_gnn_W_lang),
        "w_grav_dram": np.ascontiguousarray(L0_gnn_W_grav),
        "w_v_dram": np.ascontiguousarray(L0_gnn_W_V),
        "w_ot_dram": np.ascontiguousarray(np.asarray(L0_gnn_W_O).T),
        "gate_dram": np.asarray(L0_gnn_gate_logit).reshape(1),
        "sigma_dram": np.asarray(L0_gnn_log_sigma).reshape(1),
        "bias_dram": np.ascontiguousarray(L1_gnn_bias),
    }
    nc = bacc.Bacc("TRN2", target_bir_lowering=False, num_devices=1)
    ins = [nc.dram_tensor(name, a.shape, mybir.dt.from_np(a.dtype), kind="ExternalInput").ap()
           for name, a in arrays.items()]
    out = nc.dram_tensor("out_dram", x.shape, mybir.dt.from_np(x.dtype), kind="ExternalOutput").ap()
    build(nc, *ins, out)
    result = run_bass_kernel_spmd(nc, [arrays], core_ids=[0])
    return result.results[0]["out_dram"]
```

```python
from contextlib import ExitStack

import concourse.bass as bass
from concourse import mybir

ALU = mybir.AluOpType
ACT = mybir.ActivationFunctionType
F32 = mybir.dt.float32
F32R = mybir.dt.float32r

P = 128
GROUP = 4
EPS = 1e-8
LN_EPS = 1e-5


def build(nc, xt_d, x_d, adj_d, wlang_d, wgrav_d, wv_d, wot_d, gate_d, sigma_d, bias_d, out_d):
    B, N, D = x_d.shape
    C = D // P
    GROUPS = B // GROUP
    LOOPS = (GROUPS - 4) // 2
    PAIR = 2 * GROUP
    assert N == P and C == GROUP and GROUPS % 2 == 0 and LOOPS >= 1

    row_at = [sum(C - k for k in range(d)) for d in range(C)]
    BLOCKS = sum(C - k for k in range(C))

    with ExitStack() as ctx:
        def sb(name, shape, dt=F32):
            return ctx.enter_context(nc.sbuf_tensor(name, shape, dt))

        def bank(name):
            return ctx.enter_context(nc.psum_tensor(name, [P, 512], F32))

        def sem(name):
            return ctx.enter_context(nc.semaphore(name))

        u_w = sb("u_w", [P, 2, 2, BLOCKS, P], F32R)
        vo_w = sb("vo_w", [P, 2, C, D], F32R)
        xt = sb("xt", [P, 2, C, GROUP * P])
        xn = sb("xn", [P, 2, GROUP, D])
        ht = sb("ht", [P, 2, 2, C, GROUP, P], F32R)
        hu = sb("hu", [P, 2, 2, C, GROUP, 2, P], F32R)
        v = sb("v", [P, 2, 2, D], F32R)
        x1 = sb("x1", [P, 2, 2, D], F32R)
        kt = sb("kt", [P, 2, 2, P], F32R)
        w1 = sb("w1", [P, 2, P], F32R)
        p_sb = sb("p_sb", [P, 2, 2 * P])
        scores = sb("scores", [P, 2 * P])
        near = sb("near", [P, P])
        gauss = sb("gauss", [P, P])
        edges = sb("edges", [P, 2, 2, P])
        kmix = sb("kmix", [P, P])
        kmat = sb("kmat", [P, P])
        res1 = sb("res1", [P, D])
        x1f = sb("x1f", [P, D])
        res2 = sb("res2", [P, 2, D])
        y = sb("y", [P, 2, D])
        half_sq = sb("half_sq", [P, 2, 2])
        sq_floor = sb("sq_floor", [P, 2])
        inv_norm = sb("inv_norm", [P, 2])
        exp_bias = sb("exp_bias", [P, 2])
        degree = sb("degree", [P, 2, 2])
        floored = sb("floored", [P, 2, 2])
        recip = sb("recip", [P, 2, 2])
        share = sb("share", [P, 2, 2])
        coef = sb("coef", [P, 2, 2])
        stats = sb("stats", [P, 2, 6])
        moments = sb("moments", [P, 2, 2, 2])
        var_eps = sb("var_eps", [P, 2, 2])
        rstd = sb("rstd", [P, 2, 2])
        shift = sb("shift", [P, 2])
        ident = sb("ident", [P, P])
        adj = sb("adj", [P, P])
        mask = sb("mask", [P, P])
        w1f = sb("w1f", [P, 2, P])
        bias = sb("bias", [P, D])
        powers = sb("powers", [P, 2, 2])
        gates = sb("gates", [P, 8])
        gate, log_sigma, e_gate, sigma, one_e, w_l, inv_s2, neg_inv_s2 = (gates[:, k:k + 1] for k in range(8))
        sig_sq = sb("sig_sq", [P, 1])

        v_ps, hu_ps = bank("v_ps"), [bank("hua_ps"), bank("hub_ps")]
        s_ps = [bank("s0_ps"), bank("s1_ps")]
        kv_ps, l1_ps, setup_ps = bank("kv_ps"), bank("l1_ps"), bank("setup_ps")

        w_in = [sem(f"w_in{k}") for k in range(4)]
        adj_in, small_in = sem("adj_in"), sem("small_in")
        xt_in = [sem("xt_in0"), sem("xt_in1")]
        xn_in = [sem("xn_in0"), sem("xn_in1")]
        y_free = [sem("y_free0"), sem("y_free1")]
        ident_set, consts_set, mask_set = sem("ident_set"), sem("consts_set"), sem("mask_set")
        w_hi, w_lo = sem("w_hi"), sem("w_lo")
        products = sem("products")
        prod_hi, prod_lo = sem("prod_hi"), sem("prod_lo")
        gate_exp, gate_ops = sem("gate_exp"), sem("gate_ops")
        w1_sum, w1_hi, w1_lo = sem("w1_sum"), sem("w1_hi"), sem("w1_lo")
        ht_hi, ht_lo = sem("ht_hi"), sem("ht_lo")
        hu_mm, hu_hi, hu_lo = ([sem(f"hu{k}_{what}") for k in range(2)] for what in ("mm", "hi", "lo"))
        v_mm, v_hi, v_lo = sem("v_mm"), sem("v_hi"), sem("v_lo")
        p_mm, p_out, diag = sem("p_mm"), sem("p_out"), sem("diag")
        floor_set, norm_set, bias_set, share_set = sem("floor_set"), sem("norm_set"), sem("bias_set"), sem("share_set")
        turned = sem("turned")
        scores_set, near_set, gauss_arg, gauss_exp = sem("scores_set"), sem("near_set"), sem("gauss_arg"), sem("gauss_exp")
        edges_l, edges_g = sem("edges_l"), sem("edges_g")
        deg_floor, deg_recip, coef_set = sem("deg_floor"), sem("deg_recip"), sem("coef_set")
        mix_l, k_set = sem("mix_l"), sem("k_set")
        kt_mm, kt_hi, kt_lo = sem("kt_mm"), sem("kt_hi"), sem("kt_lo")
        kv_mm, res1_set, stats1, moments1 = sem("kv_mm"), sem("res1_set"), sem("stats1"), sem("moments1")
        x1_set, x1_hi, x1_lo = sem("x1_set"), sem("x1_hi"), sem("x1_lo")
        l1_mm, res2_set, stats2, moments2 = sem("l1_mm"), sem("res2_set"), sem("stats2"), sem("moments2")
        var_set, rstd_set, shift_set, y_set = sem("var_set"), sem("rstd_set"), sem("shift_set"), sem("y_set")

        xt_groups = xt_d
        xn_groups = x_d.rearrange("(g b) n d -> g n b d", b=GROUP)

        w_raw = [xt[:, 0], xt[:, 1], xn[:, 0], xn[:, 1]]
        w_dram = [wlang_d, wgrav_d, wv_d, wot_d]
        hu_flat = [hu[:, k].rearrange("p g c b l n -> p (g c b l n)") for k in range(2)]

        def w_split(part, k, e):
            at = (k * C + e) * D
            return hu_flat[part][:, at:at + D]

        set_a = [kv_ps, l1_ps, s_ps[0], s_ps[1]]
        set_b = [v_ps, hu_ps[0], hu_ps[1], setup_ps]
        PRODUCTS = [(0, 0, set_a, "l"), (1, 1, set_b, "g"), (2, 3, set_a, "vo")]

        def product_row(n, d):
            left, right, banks, kind = PRODUCTS[n]
            if kind == "vo":
                return banks[d][:, :], [vo_w[:, part, d, :] for part in range(2)], D
            width = (C - d) * P
            parts = [u_w[:, part, n, row_at[d]:row_at[d] + C - d, :].rearrange("p k n -> p (k n)")
                     for part in range(2)]
            return banks[d][:, 0:width], parts, width

        def raw_chunk(m):
            g, c = (m // C) % 2, m % C
            return xt[:, g, c, :], [ht[:, part, g, c, :, :].rearrange("p b n -> p (b n)") for part in range(2)]

        UNITS = [((0, 1), (0, 2)), ((1, 1), (1, 2)), ((0, 0), (0, 3)), ((1, 0), (1, 3))]

        def unit(m, k):
            kind, c = UNITS[m % C][k]
            return kind, c, m - m % C + c + 1

        def hu_out(part, m, k):
            kind, c, _ = unit(m, k)
            return hu[:, part, (m // C) % 2, c, :, kind, :]

        def ht_chunk(m, c):
            q = {(3, 0): m + 5, (3, 1): m + 6, (3, 2): m + 7, (1, 0): m + 6}.get((m % C, c), B)
            return q if q < B else None

        def by_graph(ap):
            return ap.rearrange("p (b n) -> p b n", n=P)

        PASSES = ((0, 0), (0, 1), (1, 0))

        def run(eng, slot):
            counts = range(B + 2 * C)
            for m in range(GROUP):
                slot(m, 0, counts)
            with eng.Fori(0, LOOPS) as t:
                n = {k: eng.snap(eng.to_reg(k + PAIR * t), min_val=k, max_val=k + PAIR * (LOOPS - 1)) 
                     for k in range(1, GROUP + PAIR + 8)}
                for m in range(GROUP, GROUP + PAIR):
                    slot(m, t, n)
            for m in range(GROUP + PAIR * LOOPS, B + 4):
                slot(m, 0, counts)

        block = ctx.enter_context(nc.Block())

        @block.sync
        def _(sp):
            for k in range(4):
                sp.dma_start(w_raw[k], w_dram[k].rearrange("(e p) d -> p e d", p=P)).then_inc(w_in[k], 16)
            sp.wait_ge(w_lo, C)
            sp.dma_start(xt[:, 0], xt_groups[0]).then_inc(xt_in[0], 16)
            sp.wait_ge(w_lo, 2 * C)
            sp.dma_start(xt[:, 1], xt_groups[1]).then_inc(xt_in[1], 16)
            sp.wait_ge(w_lo, 3 * C)
            sp.dma_start(xn[:, 0], xn_groups[0]).then_inc(xn_in[0], 16)
            sp.wait_ge(w_lo, 4 * C)
            sp.dma_start(xn[:, 1], xn_groups[1]).then_inc(xn_in[1], 16)

            sp.wait_ge(ht_lo, C)
            sp.dma_start(xt[:, 0], xt_groups[2]).then_inc(xt_in[0], 16)

            def slot(m, t, n):
                group = m // C + 3
                if m % C == 2 and group < GROUPS:
                    sp.wait_ge(ht_lo, n[m + 6])
                    sp.dma_start(xt[:, group % 2], xt_groups[group + 2 * t]).then_inc(xt_in[group % 2], 16)
                group = (m + 3) // C
                if m % C == 1 and 2 <= group < GROUPS:
                    sp.wait_ge(res1_set, n[m - 1])
                    sp.dma_start(xn[:, group % 2], xn_groups[group + 2 * t]).then_inc(xn_in[group % 2], 16)
                if m >= 4:
                    sp.wait_ge(y_set, n[m - 3])
                    sp.dma_start(out_d[m - 4 + PAIR * t], y[:, m % 2, :]).then_inc(y_free[m % 2], 16)

            run(sp, slot)
            for k in range(2):
                sp.wait_ge(y_free[k], 16 + 16 * (B // 2))

        @block.tensor
        def _(pe):
            for n, (left, right, banks, kind) in enumerate(PRODUCTS):
                if n == 2:
                    pe.wait_ge(prod_lo, C)
                for e in range(C):
                    pe.wait_ge(w_lo, right * C + e + 1)
                    for d in range(C):
                        out, _, width = product_row(n, d)
                        for a, b in PASSES:
                            mm = pe.matmul(out, w_split(a, left, e)[:, d * P:(d + 1) * P],
                                           w_split(b, right, e)[:, D - width:D],
                                           start=(e == 0 and (a, b) == PASSES[0]),
                                           stop=(e == C - 1 and (a, b) == PASSES[-1]))
                mm.then_inc(products, 1)

            def project(m, k):
                kind, c, _ = unit(m, k)
                for d in range(c + 1):
                    for a, b in PASSES:
                        mm = pe.matmul(hu_ps[k][:, :], u_w[:, a, kind, row_at[d] + c - d, :],
                                       ht[:, b, (m // C) % 2, d, :, :],
                                       start=(d == 0 and (a, b) == PASSES[0]),
                                       stop=(d == c and (a, b) == PASSES[-1]))
                mm.then_inc(hu_mm[k], 1)

            def values(m):
                for c in range(C):
                    for a, b in PASSES:
                        mm = pe.matmul(v_ps[:, :], ht[:, a, (m // GROUP) % 2, c, m % GROUP, :], vo_w[:, b, c, :],
                                       start=(c == 0 and (a, b) == PASSES[0]),
                                       stop=(c == C - 1 and (a, b) == PASSES[-1]))
                return mm

            pe.wait_ge(prod_lo, 2 * C)
            for m in range(C):
                for k in range(2):
                    pe.wait_ge(ht_lo, unit(m, k)[2])
                    if m > 0:
                        pe.wait_ge(hu_lo[k], m)
                    project(m, k)
            pe.wait_ge(prod_lo, 3 * C)
            values(0).then_inc(v_mm, 1)
            pe.wait_ge(ident_set, 3)
            pe.wait_ge(w1_lo, 1)

            def slot(m, t, n):
                s = s_ps[m % 2]
                if 2 <= m <= B + 1:
                    pe.wait_ge(v_lo, n[m - 1])
                    pe.wait_ge(kt_lo, n[m - 1])
                    if m >= 3:
                        pe.wait_ge(res1_set, n[m - 2])
                    for a, b in PASSES:
                        mm = pe.matmul(kv_ps[:, :], kt[:, a, m % 2, :], v[:, b, m % 2, :],
                                       start=(a, b) == PASSES[0], stop=(a, b) == PASSES[-1])
                    mm.then_inc(kv_mm, 1)
                if m < B:
                    if m % GROUP == 0:
                        pe.wait_ge(hu_lo[0], n[m + GROUP])
                        pe.wait_ge(hu_lo[1], n[m + GROUP])
                    for c in range(C):
                        for a, b in PASSES:
                            mm = pe.matmul(s[:, 0:2 * P], ht[:, a, (m // GROUP) % 2, c, m % GROUP, :],
                                           hu[:, b, (m // GROUP) % 2, c, m % GROUP, :, :],
                                           start=(c == 0 and (a, b) == PASSES[0]),
                                           stop=(c == C - 1 and (a, b) == PASSES[-1]))
                    mm.then_inc(p_mm, 1)
                if m < B - GROUP:
                    pe.wait_ge(ht_lo, n[unit(m + C, 0)[2]])
                    pe.wait_ge(hu_lo[0], n[m + 4])
                    project(m + C, 0)
                if 3 <= m <= B + 2:
                    pe.wait_ge(x1_lo, n[m - 2])
                    if m >= 4:
                        pe.wait_ge(res2_set, n[m - 3])
                    for a, b in PASSES:
                        mm = pe.matmul(l1_ps[:, :], w1[:, a, :], x1[:, b, (m - 3) % 2, :],
                                       start=(a, b) == PASSES[0], stop=(a, b) == PASSES[-1])
                    mm.then_inc(l1_mm, 1)
                if m < B - GROUP:
                    pe.wait_ge(ht_lo, n[unit(m + C, 1)[2]])
                    pe.wait_ge(hu_lo[1], n[m + 4])
                    project(m + C, 1)
                if m < B:
                    pe.wait_ge(p_out, n[m + 1])
                    pe.transpose(s[:, 0:P], p_sb[:, m % 2, 0:P], ident[:, :])
                    pe.transpose(s[:, P:2 * P], p_sb[:, m % 2, P:2 * P], ident[:, :])
                    pe.wait_ge(diag, n[m + 1])
                    pe.transpose(s[:, 3 * P:4 * P], half_sq[:, m % 2, 1:2].broadcast_to([P, P]), ident[:, :])
                    pe.wait_ge(norm_set, n[m + 1])
                    pe.transpose(s[:, 2 * P:3 * P], inv_norm[:, m % 2:m % 2 + 1].broadcast_to([P, P]),
                                 ident[:, :]).then_inc(turned, 1)
                if 1 <= m <= B:
                    pe.wait_ge(k_set, n[m])
                    pe.transpose(s_ps[(m - 1) % 2][:, 0:P], kmat[:, :], ident[:, :]).then_inc(kt_mm, 1)
                if m + 1 < B:
                    pe.wait_ge(v_lo, n[m + 1])
                    values(m + 1).then_inc(v_mm, 1)

            run(pe, slot)

        @block.scalar
        def _(act):
            act.dma_start(adj[:, :], adj_d).then_inc(adj_in, 16)
            act.dma_start(gate, gate_d.partition_broadcast(P)).then_inc(small_in, 16)
            act.dma_start(log_sigma, sigma_d.partition_broadcast(P)).then_inc(small_in, 16)
            act.dma_start(bias[:, :], bias_d.partition_broadcast(P)).then_inc(small_in, 16)

            def split_weight(k):
                for e in range(C):
                    if e == 0:
                        act.wait_ge(w_in[k], 16)
                    act.activation(w_split(0, k, e), w_raw[k][:, e, :], ACT.Copy).then_inc(w_hi, 1)

            def split_product(n):
                act.wait_ge(products, n + 1)
                for d in range(C):
                    ps, (hi, _), width = product_row(n, d)
                    if n < 2:
                        act.activation(hi[:, 0:P], ps[:, 0:P], ACT.Copy, scale=0.5)
                        if width > P:
                            act.activation(hi[:, P:width], ps[:, P:width], ACT.Copy)
                    else:
                        act.activation(hi, ps, ACT.Copy)
                    act.drain().then_inc(prod_hi, 1)

            def split_ht(m):
                raw, (hi, _) = raw_chunk(m)
                act.activation(hi, raw, ACT.Copy).then_inc(ht_hi, 1)

            for k in range(2):
                act.drain().then_inc(y_free[k], 16)
            split_weight(0)
            split_weight(1)
            split_product(0)
            split_weight(2)
            split_weight(3)
            act.wait_ge(small_in, 48)
            act.activation(e_gate, gate, ACT.Exp, scale=-1.0).then_inc(gate_exp, 1)
            act.activation(sigma, log_sigma, ACT.Exp).then_inc(gate_exp, 1)
            act.wait_ge(w1_sum, 2)
            act.activation(w1[:, 0, :], w1f[:, 1, :], ACT.Copy).then_inc(w1_hi, 1)
            act.wait_ge(xt_in[0], 16)
            for q in range(C):
                split_ht(q)
            split_product(1)
            act.wait_ge(xt_in[1], 16)
            for q in (C, C + 1, C + 2):
                split_ht(q)
            split_product(2)
            for m in range(C):
                for k in range(2):
                    act.wait_ge(hu_mm[k], m + 1)
                    act.activation(hu_out(0, m, k), by_graph(hu_ps[k][:, :]), ACT.Copy).then_inc(hu_hi[k], 1)

            def slot(m, t, n):
                def split_next(c):
                    q = ht_chunk(m, c)
                    if q is not None:
                        if q % C == 0:
                            group = q // C
                            act.wait_ge(xt_in[group % 2], 16 * (group // 2 + 1) + 16 * t)
                        split_ht(q)

                if m < B:
                    act.wait_ge(p_mm, n[m + 1])
                    act.activation(p_sb[:, m % 2, :], s_ps[m % 2][:, 0:2 * P], ACT.Copy).then_inc(p_out, 1)
                    act.wait_ge(v_mm, n[m + 1])
                    act.activation(v[:, 0, m % 2, :], v_ps[:, :], ACT.Copy).then_inc(v_hi, 1)
                split_next(0)
                if m >= 4:
                    act.wait_ge(shift_set, n[m - 3])
                    act.wait_ge(y_free[m % 2], 16 * (m // 2 - 1) + 16 * GROUP * t)
                    act.activation(y[:, m % 2, :], res2[:, m % 2, :], ACT.Identity,
                                   scale=rstd[:, (m - 1) % 2, 1:2],
                                   bias=shift[:, (m - 1) % 2:(m - 1) % 2 + 1]).then_inc(y_set, 1)
                split_next(1)
                if 1 <= m <= B:
                    act.wait_ge(kt_mm, n[m])
                    act.activation(kt[:, 0, (m - 1) % 2, :], s_ps[(m - 1) % 2][:, 0:P], ACT.Copy).then_inc(kt_hi, 1)
                if m < B - GROUP:
                    act.wait_ge(hu_mm[1], n[m + 5])
                    act.activation(hu_out(0, m + C, 1), by_graph(hu_ps[1][:, :]), ACT.Copy).then_inc(hu_hi[1], 1)
                if m < B:
                    act.wait_ge(gauss_arg, n[m + 1])
                    act.wait_ge(bias_set, n[m + 1])
                    act.activation(gauss[:, :], near[:, :], ACT.Exp, scale=inv_s2,
                                   bias=exp_bias[:, m % 2:m % 2 + 1]).then_inc(gauss_exp, 1)
                if m < B - GROUP:
                    act.wait_ge(hu_mm[0], n[m + 5])
                    act.activation(hu_out(0, m + C, 0), by_graph(hu_ps[0][:, :]), ACT.Copy).then_inc(hu_hi[0], 1)
                split_next(2)
                if 2 <= m <= B + 1:
                    act.wait_ge(x1_set, n[m - 1])
                    act.activation(x1[:, 0, m % 2, :], x1f[:, :], ACT.Copy).then_inc(x1_hi, 1)

            run(act, slot)

        @block.vector
        def _(dve):
            def rest(out, full, hi):
                return dve.tensor_tensor(out, full, hi.bitcast(F32), ALU.subtract)

            def split_weight(k):
                for e in range(C):
                    dve.wait_ge(w_hi, k * C + e + 1)
                    rest(w_split(1, k, e), w_raw[k][:, e, :], w_split(0, k, e)).then_inc(w_lo, 1)

            def split_product(n):
                for d in range(C):
                    dve.wait_ge(prod_hi, n * C + d + 1)
                    ps, (hi, lo), width = product_row(n, d)
                    if n < 2:
                        last = dve.scalar_tensor_tensor(lo[:, 0:P], ps[:, 0:P], 0.5, hi[:, 0:P].bitcast(F32),
                                                        ALU.mult, ALU.subtract)
                        if width > P:
                            last = rest(lo[:, P:width], ps[:, P:width], hi[:, P:width])
                    else:
                        last = rest(lo, ps, hi)
                    last.then_inc(prod_lo, 1)

            dve.wait_ge(adj_in, 16)
            dve.tensor_tensor(w1f[:, 0, :], adj[:, :], adj[:, :], ALU.mult).then_inc(w1_sum, 1)
            dve.wait_ge(w1_sum, 1)
            dve.wait_ge(ident_set, 3)
            dve.tensor_tensor(w1f[:, 1, :], w1f[:, 0, :], ident[:, :], ALU.add).then_inc(w1_sum, 1)
            split_weight(0)
            split_weight(1)
            split_product(0)
            split_weight(2)
            split_weight(3)
            dve.wait_ge(w1_hi, 1)
            rest(w1[:, 1, :], w1f[:, 1, :], w1[:, 0, :]).then_inc(w1_lo, 1)
            dve.wait_ge(gate_exp, 2)
            dve.tensor_scalar(one_e, e_gate, 1.0, None, ALU.add).then_inc(gate_ops, 1)
            dve.tensor_tensor(sig_sq[:, :], sigma, sigma, ALU.mult).then_inc(gate_ops, 1)
            dve.wait_ge(gate_ops, 2)
            dve.reciprocal(w_l, one_e).then_inc(gate_ops, 1)
            dve.reciprocal(inv_s2, sig_sq[:, :]).then_inc(gate_ops, 1)
            dve.wait_ge(gate_ops, 4)
            dve.tensor_scalar(neg_inv_s2, inv_s2, -1.0, None, ALU.mult).then_inc(gate_ops, 1)
            for k in range(2):
                dve.tensor_scalar(share[:, k, 1:2], w_l, -1.0, 1.0, ALU.mult, ALU.add).then_inc(gate_ops, 1)
            split_product(1)
            split_product(2)
            for m in range(C):
                for k in range(2):
                    dve.wait_ge(hu_hi[k], m + 1)
                    rest(hu_out(1, m, k), by_graph(hu_ps[k][:, :]), hu_out(0, m, k)).then_inc(hu_lo[k], 1)
            dve.wait_ge(mask_set, 1)

            def slot(m, t, n):
                q = (m - 1) % 2
                s = s_ps[m % 2]
                if m < B:
                    dve.wait_ge(p_out, n[m + 1])
                    for k in range(2):
                        last = dve.tensor_tensor_reduce(scores[:, k * P:(k + 1) * P], p_sb[:, m % 2, k * P:(k + 1) * P],
                                                        ident[:, :], 1.0, 0.0, ALU.mult, ALU.add,
                                                        half_sq[:, m % 2, k:k + 1])
                    last.then_inc(diag, 1)
                if 1 <= m <= B:
                    dve.wait_ge(coef_set, n[m])
                    dve.tensor_scalar(kmix[:, :], edges[:, q, 0, :], coef[:, q, 0:1], None, ALU.mult).then_inc(mix_l, 1)
                if m < B:
                    dve.wait_ge(v_hi, n[m + 1])
                    rest(v[:, 1, m % 2, :], v_ps[:, :], v[:, 0, m % 2, :]).then_inc(v_lo, 1)
                if 1 <= m <= B:
                    dve.wait_ge(mix_l, n[m])
                    dve.scalar_tensor_tensor(kmat[:, :], edges[:, q, 1, :], coef[:, q, 1:2], kmix[:, :],
                                             ALU.mult, ALU.add).then_inc(k_set, 1)
                if 3 <= m <= B + 2:
                    dve.wait_ge(l1_mm, n[m - 2])
                    if m >= B:
                        dve.wait_ge(y_set, n[m - 4])
                    dve.tensor_tensor(res2[:, (m - 3) % 2, :], l1_ps[:, :], bias[:, :], ALU.add).then_inc(res2_set, 1)
                if 2 <= m <= B + 1:
                    dve.wait_ge(ident_set, 1)
                    dve.wait_ge(stats1, n[m - 1])
                    dve.bn_aggr(moments[:, m % 2, 0, :], stats[:, 0, :]).then_inc(moments1, 1)
                if 3 <= m <= B + 2:
                    dve.wait_ge(res2_set, n[m - 2])
                    dve.bn_stats(stats[:, 1, :], res2[:, (m - 3) % 2, :]).then_inc(stats2, 1)
                    dve.wait_ge(ident_set, 1)
                    dve.wait_ge(stats2, n[m - 2])
                    dve.bn_aggr(moments[:, m % 2, 1, :], stats[:, 1, :]).then_inc(moments2, 1)
                if m < B:
                    dve.wait_ge(turned, n[m + 1])
                    dve.wait_ge(diag, n[m + 1])
                    dve.tensor_tensor(scores[:, :], s[:, 0:2 * P], p_sb[:, m % 2, :], ALU.add).then_inc(scores_set, 1)
                    dve.tensor_tensor(edges[:, m % 2, 1, :], s[:, 2 * P:3 * P], mask[:, :], ALU.mult).then_inc(near_set, 1)
                    dve.wait_ge(scores_set, n[m + 1])
                    dve.tensor_tensor(near[:, :], scores[:, P:2 * P], s[:, 3 * P:4 * P], ALU.subtract).then_inc(gauss_arg, 1)
                if 1 <= m <= B:
                    dve.wait_ge(kt_hi, n[m])
                    rest(kt[:, 1, q, :], s_ps[q][:, 0:P], kt[:, 0, q, :]).then_inc(kt_lo, 1)
                if m < B - GROUP:
                    dve.wait_ge(hu_hi[1], n[m + 5])
                    rest(hu_out(1, m + C, 1), by_graph(hu_ps[1][:, :]), hu_out(0, m + C, 1)).then_inc(hu_lo[1], 1)
                if m < B:
                    dve.wait_ge(near_set, n[m + 1])
                    dve.scalar_tensor_tensor(edges[:, m % 2, 0, :], scores[:, 0:P], 0.0, edges[:, m % 2, 1, :],
                                             ALU.max, ALU.mult, accum_out=degree[:, m % 2, 0:1]).then_inc(edges_l, 1)
                if 2 <= m <= B + 1:
                    dve.wait_ge(rstd_set, n[m - 1])
                    dve.tensor_scalar(x1f[:, :], res1[:, :], moments[:, m % 2, 0, 0:1], rstd[:, m % 2, 0:1],
                                      ALU.subtract, ALU.mult).then_inc(x1_set, 1)
                if m < B - GROUP:
                    dve.wait_ge(hu_hi[0], n[m + 5])
                    rest(hu_out(1, m + C, 0), by_graph(hu_ps[0][:, :]), hu_out(0, m + C, 0)).then_inc(hu_lo[0], 1)
                if m < B:
                    dve.wait_ge(gauss_exp, n[m + 1])
                    dve.wait_ge(edges_l, n[m + 1])
                    dve.scalar_tensor_tensor(edges[:, m % 2, 1, :], gauss[:, :], 1.0, mask[:, :],
                                             ALU.min, ALU.mult, accum_out=degree[:, m % 2, 1:2]).then_inc(edges_g, 1)
                if 1 <= m <= B:
                    dve.wait_ge(kv_mm, n[m])
                    if m >= 2:
                        dve.wait_ge(x1_set, n[m - 1])
                    if (m - 1) % GROUP == 0:
                        group = (m - 1) // GROUP
                        dve.wait_ge(xn_in[group % 2], 16 * (group // 2 + 1) + 16 * t)
                    dve.tensor_tensor(res1[:, :], kv_ps[:, :], xn[:, ((m - 1) // GROUP) % 2, (m - 1) % GROUP, :],
                                      ALU.add).then_inc(res1_set, 1)
                if 2 <= m <= B + 1:
                    dve.wait_ge(x1_hi, n[m - 1])
                    rest(x1[:, 1, m % 2, :], x1f[:, :], x1[:, 0, m % 2, :]).then_inc(x1_lo, 1)
                if 1 <= m <= B:
                    dve.wait_ge(res1_set, n[m])
                    dve.bn_stats(stats[:, 0, :], res1[:, :]).then_inc(stats1, 1)

            run(dve, slot)

        @block.gpsimd
        def _(pool):
            pool.memset(ident[:, :], 0.0).then_inc(ident_set, 1)
            pool.memset(powers[:, 0, :], -0.5).then_inc(consts_set, 1)
            pool.memset(powers[:, 1, :], -1.0).then_inc(consts_set, 1)
            pool.wait_ge(ident_set, 1)
            pool.affine_select(out=ident[:, :], in_=ident[:, :], compare_op=ALU.not_equal, fill=1.0, base=0,
                               pattern=[[-1, P]], channel_multiplier=1).then_inc(ident_set, 2)
            pool.wait_ge(adj_in, 16)
            pool.affine_select(out=mask[:, :], in_=adj[:, :], compare_op=ALU.not_equal, fill=0.0, base=0,
                               pattern=[[-1, P]], channel_multiplier=1).then_inc(mask_set, 1)

            def split_ht(m):
                raw, (hi, lo) = raw_chunk(m)
                pool.tensor_tensor(lo, raw, hi.bitcast(F32), ALU.subtract).then_inc(ht_lo, 1)

            for q in [*range(C), *(C, C + 1, C + 2)]:
                pool.wait_ge(ht_hi, q + 1)
                split_ht(q)
            pool.wait_ge(consts_set, 2)
            pool.wait_ge(gate_ops, 7)

            def slot(m, t, n):
                p = m % 2

                def split_next(c):
                    q = ht_chunk(m, c)
                    if q is not None:
                        pool.wait_ge(ht_hi, n[q + 1])
                        split_ht(q)

                split_next(0)
                if m < B:
                    pool.wait_ge(ident_set, 1)
                    pool.wait_ge(diag, n[m + 1])
                    pool.tensor_scalar(sq_floor[:, p:p + 1], half_sq[:, p, 0:1], 2.0, EPS * EPS,
                                       ALU.mult, ALU.max).then_inc(floor_set, 1)
                    pool.wait_ge(floor_set, n[m + 1])
                    pool.tensor_tensor(inv_norm[:, p:p + 1], sq_floor[:, p:p + 1], powers[:, 0, 0:1],
                                       ALU.pow).then_inc(norm_set, 1)
                    pool.tensor_scalar(exp_bias[:, p:p + 1], half_sq[:, p, 1:2], neg_inv_s2, None,
                                       ALU.mult).then_inc(bias_set, 1)
                    pool.wait_ge(ident_set, 1)
                    pool.wait_ge(norm_set, n[m + 1])
                    pool.tensor_scalar(share[:, p, 0:1], inv_norm[:, p:p + 1], w_l, None, ALU.mult).then_inc(share_set, 1)
                if 2 <= m <= B + 2:
                    a, b = (0 if m <= B + 1 else 1), (2 if m >= 3 else 1)
                    pool.wait_ge(ident_set, 1)
                    if m <= B + 1:
                        pool.wait_ge(moments1, n[m - 1])
                    if m >= 3:
                        pool.wait_ge(moments2, n[m - 2])
                    pool.tensor_scalar(var_eps[:, p, a:b], moments[:, p, a:b, 1], LN_EPS, None, ALU.add).then_inc(var_set, 1)
                    pool.wait_ge(var_set, n[m - 1])
                    pool.tensor_tensor(rstd[:, p, a:b], var_eps[:, p, a:b], powers[:, 0, a:b], ALU.pow).then_inc(rstd_set, 1)
                split_next(1)
                if m < B:
                    pool.wait_ge(ident_set, 1)
                    pool.wait_ge(edges_l, n[m + 1])
                    pool.tensor_scalar(floored[:, p, 0:1], degree[:, p, 0:1], inv_norm[:, p:p + 1], EPS,
                                       ALU.mult, ALU.max)
                    pool.wait_ge(ident_set, 1)
                    pool.wait_ge(edges_g, n[m + 1])
                    pool.tensor_scalar(floored[:, p, 1:2], degree[:, p, 1:2], EPS, None, ALU.max).then_inc(deg_floor, 1)
                if 3 <= m <= B + 2:
                    pool.wait_ge(ident_set, 1)
                    pool.wait_ge(rstd_set, n[m - 1])
                    pool.tensor_scalar(shift[:, p:p + 1], moments[:, p, 1, 0:1], -1.0, rstd[:, p, 1:2],
                                       ALU.mult, ALU.mult).then_inc(shift_set, 1)
                if m < B:
                    pool.wait_ge(deg_floor, n[m + 1])
                    pool.tensor_tensor(recip[:, p, :], floored[:, p, :], powers[:, 1, :], ALU.pow).then_inc(deg_recip, 1)
                split_next(2)
                if m < B:
                    pool.wait_ge(deg_recip, n[m + 1])
                    pool.wait_ge(share_set, n[m + 1])
                    pool.tensor_tensor(coef[:, p, :], recip[:, p, :], share[:, p, :], ALU.mult).then_inc(coef_set, 1)

            run(pool, slot)


def kernel(x, adj, L0_gnn_W_lang, L0_gnn_W_grav, L0_gnn_W_V, L0_gnn_W_O, L0_gnn_gate_logit, L0_gnn_log_sigma,
           L1_gnn_bias):
    import numpy as np
    import concourse.bacc as bacc
    from concourse.bass_utils import run_bass_kernel_spmd

    x = np.asarray(x)
    batch, nodes, dim = x.shape
    xt = x.reshape(batch // GROUP, GROUP, nodes, dim // P, P).transpose(0, 4, 3, 1, 2)
    arrays = {
        "xt_dram": np.ascontiguousarray(xt).reshape(batch // GROUP, P, dim // P, GROUP * nodes),
        "x_dram": np.ascontiguousarray(x),
        "adj_dram": np.ascontiguousarray(adj),
        "w_lang_dram": np.ascontiguousarray(L0_gnn_W_lang),
        "w_grav_dram": np.ascontiguousarray(L0_gnn_W_grav),
        "w_v_dram": np.ascontiguousarray(L0_gnn_W_V),
        "w_ot_dram": np.ascontiguousarray(np.asarray(L0_gnn_W_O).T),
        "gate_dram": np.asarray(L0_gnn_gate_logit).reshape(1),
        "sigma_dram": np.asarray(L0_gnn_log_sigma).reshape(1),
        "bias_dram": np.ascontiguousarray(L1_gnn_bias),
    }
    nc = bacc.Bacc("TRN2", target_bir_lowering=False, num_devices=1)
    ins = [nc.dram_tensor(name, a.shape, mybir.dt.from_np(a.dtype), kind="ExternalInput").ap()
           for name, a in arrays.items()]
    out = nc.dram_tensor("out_dram", x.shape, mybir.dt.from_np(x.dtype), kind="ExternalOutput").ap()
    build(nc, *ins, out)
    result = run_bass_kernel_spmd(nc, [arrays], core_ids=[0])
    return result.results[0]["out_dram"]
```

```python
from contextlib import ExitStack

import concourse.bass as bass
from concourse import mybir

ALU = mybir.AluOpType
ACT = mybir.ActivationFunctionType
F32 = mybir.dt.float32
F32R = mybir.dt.float32r

P = 128
GROUP = 4
EPS = 1e-8
LN_EPS = 1e-5
WARM_UP = 6


def build(nc, xt_d, x_d, adj_d, wlang_d, wgrav_d, wv_d, wot_d, gate_d, sigma_d, bias_d, out_d):
    B, N, D = x_d.shape
    C = D // P
    GROUPS = B // GROUP
    LOOPS = (GROUPS - 4) // 2
    PAIR = 2 * GROUP
    assert N == P and C == GROUP and GROUPS % 2 == 0 and LOOPS >= 1

    row_at = [sum(C - k for k in range(d)) for d in range(C)]
    BLOCKS = sum(C - k for k in range(C))

    with ExitStack() as ctx:
        def sb(name, shape, dt=F32):
            return ctx.enter_context(nc.sbuf_tensor(name, shape, dt))

        def bank(name):
            return ctx.enter_context(nc.psum_tensor(name, [P, 512], F32))

        def sem(name):
            return ctx.enter_context(nc.semaphore(name))

        u_w = sb("u_w", [P, 2, 2, BLOCKS, P], F32R)
        vo_w = sb("vo_w", [P, 2, C, D], F32R)
        xt = sb("xt", [P, 2, C, GROUP * P])
        xn = sb("xn", [P, 2, GROUP, D])
        ht = sb("ht", [P, 2, 2, C, GROUP, P], F32R)
        hu = sb("hu", [P, 2, 2, C, GROUP, 2, P], F32R)
        v = sb("v", [P, 2, 2, D], F32R)
        x1 = sb("x1", [P, 2, 2, D], F32R)
        kt = sb("kt", [P, 2, 2, P], F32R)
        w1 = sb("w1", [P, 2, P], F32R)
        p_sb = sb("p_sb", [P, 2, 2 * P])
        p_down = sb("p_down", [P, P])
        scores = sb("scores", [P, P])
        near = sb("near", [P, P])
        gauss = sb("gauss", [P, P])
        edges = sb("edges", [P, 2, 2, P])
        kmix = sb("kmix", [P, P])
        kmat = sb("kmat", [P, P])
        res1 = sb("res1", [P, D])
        x1f = sb("x1f", [P, D])
        res2 = sb("res2", [P, 2, D])
        y = sb("y", [P, 2, D])
        half_sq = sb("half_sq", [P, 2])
        neg_half_sq = sb("neg_half_sq", [P, 2])
        sq_floor = sb("sq_floor", [P, 2])
        inv_norm = sb("inv_norm", [P, 2])
        exp_bias = sb("exp_bias", [P, 2])
        degree = sb("degree", [P, 2, 2])
        floored = sb("floored", [P, 2, 2])
        recip = sb("recip", [P, 2, 2])
        share = sb("share", [P, 2, 2])
        coef = sb("coef", [P, 2, 2])
        stats = sb("stats", [P, 2, 6])
        moments = sb("moments", [P, 2, 2, 2])
        var_eps = sb("var_eps", [P, 2, 2])
        rstd = sb("rstd", [P, 2, 2])
        shift = sb("shift", [P, 2])
        ident = sb("ident", [P, P])
        adj = sb("adj", [P, P])
        mask = sb("mask", [P, P])
        w1f = sb("w1f", [P, 2, P])
        bias = sb("bias", [P, D])
        powers = sb("powers", [P, 2, 2])
        gates = sb("gates", [P, 7])
        gate, log_sigma, e_gate, sigma, one_e, w_l, inv_s2 = (gates[:, k:k + 1] for k in range(7))
        sig_sq = sb("sig_sq", [P, 1])

        v_ps, hu_ps = bank("v_ps"), [bank("hu0_ps"), bank("hu1_ps")]
        s_ps = [bank("s0_ps"), bank("s1_ps")]
        kv_ps, l1_ps, setup_ps = bank("kv_ps"), bank("l1_ps"), bank("setup_ps")

        wlang_in = [sem(f"wlang_in{e}") for e in range(C)]
        w_in = [sem(f"w_in{k}") for k in range(3)]
        adj_in, small_in = sem("adj_in"), sem("small_in")
        xt_in = [sem("xt_in0"), sem("xt_in1")]
        xn_in = [sem("xn_in0"), sem("xn_in1")]
        y_free = [sem("y_free0"), sem("y_free1")]
        zeros_set = sem("zeros_set")
        ident_set, consts_set, mask_set = sem("ident_set"), sem("consts_set"), sem("mask_set")
        w_hi, w_lo = sem("w_hi"), sem("w_lo")
        products = sem("products")
        prod_hi, prod_lo = sem("prod_hi"), sem("prod_lo")
        gate_exp, gate_ops = sem("gate_exp"), sem("gate_ops")
        w1_sum, w1_hi, w1_lo = sem("w1_sum"), sem("w1_hi"), sem("w1_lo")
        ht_hi, ht_lo = sem("ht_hi"), sem("ht_lo")
        hu_mm, hu_hi, hu_lo = ([sem(f"hu{k}_{what}") for k in range(2)] for what in ("mm", "hi", "lo"))
        v_mm, v_hi, v_lo = sem("v_mm"), sem("v_hi"), sem("v_lo")
        p_mm, p_out, diag, p_down_set = sem("p_mm"), sem("p_out"), sem("diag"), sem("p_down_set")
        floor_set, norm_set, bias_set, share_set = sem("floor_set"), sem("norm_set"), sem("bias_set"), sem("share_set")
        turned = sem("turned")
        scores_set, over_norm, gauss_arg, gauss_exp = sem("scores_set"), sem("over_norm"), sem("gauss_arg"), sem("gauss_exp")
        edges_l, edges_g = sem("edges_l"), sem("edges_g")
        deg_floor, deg_recip, coef_set = sem("deg_floor"), sem("deg_recip"), sem("coef_set")
        mix_l, k_set = sem("mix_l"), sem("k_set")
        kt_mm, kt_hi, kt_lo = sem("kt_mm"), sem("kt_hi"), sem("kt_lo")
        kv_mm, res1_set, stats1, moments1 = sem("kv_mm"), sem("res1_set"), sem("stats1"), sem("moments1")
        x1_set, x1_hi, x1_lo = sem("x1_set"), sem("x1_hi"), sem("x1_lo")
        l1_mm, res2_set, stats2, moments2 = sem("l1_mm"), sem("res2_set"), sem("stats2"), sem("moments2")
        var_set, rstd_set, shift_set, y_set = sem("var_set"), sem("rstd_set"), sem("shift_set"), sem("y_set")

        xn_groups = x_d.rearrange("(g b) n d -> g n b d", b=GROUP)

        w_raw = [xt[:, 0], xt[:, 1], xn[:, 0], xn[:, 1]]
        w_dram = [wlang_d, wgrav_d, wv_d, wot_d]
        hu_flat = [hu[:, k].rearrange("p g c b l n -> p (g c b l n)") for k in range(2)]

        def w_split(part, k, e):
            at = (k * C + e) * D
            return hu_flat[part][:, at:at + D]

        set_a = [kv_ps, l1_ps, s_ps[0], s_ps[1]]
        set_b = [v_ps, hu_ps[0], hu_ps[1], setup_ps]
        PRODUCTS = [(0, 0, set_a, "l"), (1, 1, set_b, "g"), (2, 3, set_a, "vo")]

        def product_row(n, d):
            left, right, banks, kind = PRODUCTS[n]
            if kind == "vo":
                return banks[d][:, :], [vo_w[:, part, d, :] for part in range(2)], D
            width = (C - d) * P
            parts = [u_w[:, part, n, row_at[d]:row_at[d] + C - d, :].rearrange("p k n -> p (k n)")
                     for part in range(2)]
            return banks[d][:, 0:width], parts, width

        def raw_chunk(m):
            g, c = (m // C) % 2, m % C
            return xt[:, g, c, :], [ht[:, part, g, c, :, :].rearrange("p b n -> p (b n)") for part in range(2)]

        UNITS = [((0, 1), (0, 2)), ((1, 1), (1, 2)), ((0, 0), (0, 3)), ((1, 0), (1, 3))]

        def unit(m, k):
            kind, c = UNITS[m % C][k]
            return kind, c, m - m % C + c + 1

        early_banks = [*hu_ps, setup_ps]

        def early_bank(m, k):
            return early_banks[(2 * m + k) % len(early_banks)]

        def hu_out(part, m, k):
            kind, c, _ = unit(m, k)
            return hu[:, part, (m // C) % 2, c, :, kind, :]

        def ht_early(m, c):
            return m + 5 + c if m % C == 3 and m + 5 < B else None

        def by_graph(ap):
            return ap.rearrange("p (b n) -> p b n", n=P)

        PASSES = ((0, 0), (0, 1), (1, 0))

        def run(eng, slot):
            counts = range(B + 2 * C)
            for m in range(GROUP):
                slot(m, 0, counts)
            with eng.Fori(0, LOOPS) as t:
                n = {k: eng.snap(eng.to_reg(k + PAIR * t), min_val=k, max_val=k + PAIR * (LOOPS - 1))
                     for k in range(1, GROUP + PAIR + 8)}
                for m in range(GROUP, GROUP + PAIR):
                    slot(m, t, n)
            for m in range(GROUP + PAIR * LOOPS, B + 4):
                slot(m, 0, counts)

        block = ctx.enter_context(nc.Block())

        @block.sync
        def _(sp):
            for e in range(C):
                sp.dma_start(w_raw[0][:, e, :], w_dram[0][e * P:(e + 1) * P, :]).then_inc(wlang_in[e], 16)
            for k in range(1, 4):
                sp.dma_start(w_raw[k], w_dram[k].rearrange("(e p) d -> p e d", p=P)).then_inc(w_in[k - 1], 16)
            sp.dma_start(adj[:, :], adj_d).then_inc(adj_in, 16)
            sp.dma_start(gate, gate_d.partition_broadcast(P)).then_inc(small_in, 16)
            sp.dma_start(log_sigma, sigma_d.partition_broadcast(P)).then_inc(small_in, 16)
            sp.dma_start(bias[:, :], bias_d.partition_broadcast(P)).then_inc(small_in, 16)
            sp.wait_ge(w_lo, C)
            sp.dma_start(xt[:, 0], xt_d[0]).then_inc(xt_in[0], 16)
            sp.wait_ge(w_lo, 2 * C)
            sp.dma_start(xt[:, 1], xt_d[1]).then_inc(xt_in[1], 16)
            sp.wait_ge(w_lo, 3 * C)
            sp.dma_start(xn[:, 0], xn_groups[0]).then_inc(xn_in[0], 16)
            sp.wait_ge(w_lo, 4 * C)
            sp.dma_start(xn[:, 1], xn_groups[1]).then_inc(xn_in[1], 16)

            sp.wait_ge(ht_lo, C)
            sp.dma_start(xt[:, 0], xt_d[2]).then_inc(xt_in[0], 16)

            def slot(m, t, n):
                group = m // C + 3
                if m % C == 2 and group < GROUPS:
                    sp.wait_ge(ht_lo, n[m + 6])
                    sp.dma_start(xt[:, group % 2], xt_d[group + 2 * t]).then_inc(xt_in[group % 2], 16)
                group = (m + 3) // C
                if m % C == 1 and 2 <= group < GROUPS:
                    sp.wait_ge(res1_set, n[m - 1])
                    sp.dma_start(xn[:, group % 2], xn_groups[group + 2 * t]).then_inc(xn_in[group % 2], 16)
                if m >= 4:
                    sp.wait_ge(y_set, n[m - 3])
                    sp.dma_start(out_d[m - 4 + PAIR * t], y[:, m % 2, :]).then_inc(y_free[m % 2], 16)

            run(sp, slot)
            for k in range(2):
                sp.wait_ge(y_free[k], 16 + 16 * (B // 2))

        @block.tensor
        def _(pe):
            pe.wait_ge(zeros_set, 1)
            for _ in range(WARM_UP):
                pe.matmul(setup_ps[:, :], x1[:, 0, 0, 0:P], x1[:, 0, 0, :], start=True, stop=True)

            for n, (left, right, banks, kind) in enumerate(PRODUCTS):
                if n == 2:
                    pe.wait_ge(prod_lo, C)
                for e in range(C):
                    for a, b in PASSES:
                        if (a, b) == (0, 0):
                            pe.wait_ge(w_hi, right * C + e + 1)
                        elif (a, b) == (0, 1):
                            pe.wait_ge(w_lo, right * C + e + 1)
                        for d in range(C):
                            out, _, width = product_row(n, d)
                            mm = pe.matmul(out, w_split(a, left, e)[:, d * P:(d + 1) * P],
                                           w_split(b, right, e)[:, D - width:D],
                                           start=(e == 0 and (a, b) == PASSES[0]),
                                           stop=(e == C - 1 and (a, b) == PASSES[-1]))
                mm.then_inc(products, 1)

            def project(m, k, ps):
                kind, c, _ = unit(m, k)
                for d in range(c + 1):
                    for a, b in PASSES:
                        mm = pe.matmul(ps[:, :], u_w[:, a, kind, row_at[d] + c - d, :],
                                       ht[:, b, (m // C) % 2, d, :, :],
                                       start=(d == 0 and (a, b) == PASSES[0]),
                                       stop=(d == c and (a, b) == PASSES[-1]))
                mm.then_inc(hu_mm[k], 1)

            def values(m):
                for c in range(C):
                    for a, b in PASSES:
                        mm = pe.matmul(v_ps[:, :], ht[:, a, (m // GROUP) % 2, c, m % GROUP, :], vo_w[:, b, c, :],
                                       start=(c == 0 and (a, b) == PASSES[0]),
                                       stop=(c == C - 1 and (a, b) == PASSES[-1]))
                return mm

            pe.wait_ge(prod_lo, 2 * C)
            for m in range(C):
                for k in range(2):
                    pe.wait_ge(ht_lo, unit(m, k)[2])
                    last = 2 * m + k - len(early_banks)
                    if last >= 0:
                        pe.wait_ge(hu_lo[last % 2], last // 2 + 1)
                    project(m, k, early_bank(m, k))
            pe.wait_ge(prod_lo, 3 * C)
            values(0).then_inc(v_mm, 1)
            pe.wait_ge(ident_set, 3)
            pe.wait_ge(w1_lo, 1)

            def slot(m, t, n):
                s = s_ps[m % 2]
                if 2 <= m <= B + 1:
                    pe.wait_ge(v_lo, n[m - 1])
                    pe.wait_ge(kt_lo, n[m - 1])
                    if m >= 3:
                        pe.wait_ge(res1_set, n[m - 2])
                    for a, b in PASSES:
                        mm = pe.matmul(kv_ps[:, :], kt[:, a, m % 2, :], v[:, b, m % 2, :],
                                       start=(a, b) == PASSES[0], stop=(a, b) == PASSES[-1])
                    mm.then_inc(kv_mm, 1)
                if m < B:
                    if m % GROUP == 0:
                        pe.wait_ge(hu_lo[0], n[m + GROUP])
                        pe.wait_ge(hu_lo[1], n[m + GROUP])
                    for c in range(C):
                        for a, b in PASSES:
                            mm = pe.matmul(s[:, 0:2 * P], ht[:, a, (m // GROUP) % 2, c, m % GROUP, :],
                                           hu[:, b, (m // GROUP) % 2, c, m % GROUP, :, :],
                                           start=(c == 0 and (a, b) == PASSES[0]),
                                           stop=(c == C - 1 and (a, b) == PASSES[-1]))
                    mm.then_inc(p_mm, 1)
                if m < B - GROUP:
                    pe.wait_ge(ht_lo, n[unit(m + C, 0)[2]])
                    pe.wait_ge(hu_lo[0], n[m + 4])
                    project(m + C, 0, hu_ps[0])
                if 3 <= m <= B + 2:
                    pe.wait_ge(x1_lo, n[m - 2])
                    if m >= 4:
                        pe.wait_ge(res2_set, n[m - 3])
                    for a, b in PASSES:
                        mm = pe.matmul(l1_ps[:, :], w1[:, a, :], x1[:, b, (m - 3) % 2, :],
                                       start=(a, b) == PASSES[0], stop=(a, b) == PASSES[-1])
                    mm.then_inc(l1_mm, 1)
                if m < B - GROUP:
                    pe.wait_ge(ht_lo, n[unit(m + C, 1)[2]])
                    pe.wait_ge(hu_lo[1], n[m + 4])
                    project(m + C, 1, hu_ps[1])
                if m < B:
                    pe.wait_ge(p_out, n[m + 1])
                    pe.transpose(s[:, 0:P], p_sb[:, m % 2, 0:P], ident[:, :])
                    pe.wait_ge(p_down_set, n[m + 1])
                    pe.transpose(s[:, P:2 * P], p_down[:, :], ident[:, :])
                    pe.wait_ge(norm_set, n[m + 1])
                    pe.transpose(s[:, 2 * P:3 * P], inv_norm[:, m % 2:m % 2 + 1].broadcast_to([P, P]),
                                 ident[:, :]).then_inc(turned, 1)
                if 1 <= m <= B:
                    pe.wait_ge(k_set, n[m])
                    pe.transpose(s_ps[(m - 1) % 2][:, 0:P], kmat[:, :], ident[:, :]).then_inc(kt_mm, 1)
                if m + 1 < B:
                    pe.wait_ge(v_lo, n[m + 1])
                    values(m + 1).then_inc(v_mm, 1)

            run(pe, slot)

        @block.scalar
        def _(act):
            def split_weight(k):
                for e in range(C):
                    if k == 0:
                        act.wait_ge(wlang_in[e], 16)
                    elif e == 0:
                        act.wait_ge(w_in[k - 1], 16)
                    act.activation(w_split(0, k, e), w_raw[k][:, e, :], ACT.Copy).then_inc(w_hi, 1)

            def split_product(n):
                act.wait_ge(products, n + 1)
                for d in range(C):
                    ps, (hi, _), width = product_row(n, d)
                    if n < 2:
                        act.activation(hi[:, 0:P], ps[:, 0:P], ACT.Copy, scale=0.5)
                        if width > P:
                            act.activation(hi[:, P:width], ps[:, P:width], ACT.Copy)
                    else:
                        act.activation(hi, ps, ACT.Copy)
                    act.drain().then_inc(prod_hi, 1)

            def split_ht(m):
                raw, (hi, _) = raw_chunk(m)
                act.activation(hi, raw, ACT.Copy).then_inc(ht_hi, 1)

            for k in range(2):
                act.drain().then_inc(y_free[k], 16)
            split_weight(0)
            split_weight(1)
            split_product(0)
            split_weight(2)
            split_weight(3)
            act.wait_ge(small_in, 48)
            act.activation(e_gate, gate, ACT.Exp, scale=-1.0).then_inc(gate_exp, 1)
            act.activation(sigma, log_sigma, ACT.Exp).then_inc(gate_exp, 1)
            act.wait_ge(w1_sum, 2)
            act.activation(w1[:, 0, :], w1f[:, 1, :], ACT.Copy).then_inc(w1_hi, 1)
            act.wait_ge(xt_in[0], 16)
            for q in range(C):
                split_ht(q)
            split_product(1)
            act.wait_ge(xt_in[1], 16)
            for q in range(C, 2 * C - 1):
                split_ht(q)
            split_product(2)
            for m in range(C):
                for k in range(2):
                    act.wait_ge(hu_mm[k], m + 1)
                    act.activation(hu_out(0, m, k), by_graph(early_bank(m, k)[:, :]), ACT.Copy).then_inc(hu_hi[k], 1)

            def slot(m, t, n):
                def split_next(c):
                    q = ht_early(m, c)
                    if q is not None:
                        if c == 0:
                            group = q // C
                            act.wait_ge(xt_in[group % 2], 16 * (group // 2 + 1) + 16 * t)
                        split_ht(q)

                if m < B:
                    act.wait_ge(p_mm, n[m + 1])
                    act.activation(p_sb[:, m % 2, :], s_ps[m % 2][:, 0:2 * P], ACT.Copy).then_inc(p_out, 1)
                    act.wait_ge(v_mm, n[m + 1])
                    act.activation(v[:, 0, m % 2, :], v_ps[:, :], ACT.Copy).then_inc(v_hi, 1)
                if m < B - GROUP:
                    act.wait_ge(hu_mm[0], n[m + 5])
                    act.activation(hu_out(0, m + C, 0), by_graph(hu_ps[0][:, :]), ACT.Copy).then_inc(hu_hi[0], 1)
                if m < B:
                    act.wait_ge(diag, n[m + 1])
                    act.activation(p_down[:, :], p_sb[:, m % 2, P:2 * P], ACT.Identity,
                                   bias=neg_half_sq[:, m % 2:m % 2 + 1]).then_inc(p_down_set, 1)
                if m >= 4:
                    act.wait_ge(shift_set, n[m - 3])
                    act.wait_ge(y_free[m % 2], 16 * (m // 2 - 1) + 16 * GROUP * t)
                    act.activation(y[:, m % 2, :], res2[:, m % 2, :], ACT.Identity,
                                   scale=rstd[:, (m - 1) % 2, 1:2],
                                   bias=shift[:, (m - 1) % 2:(m - 1) % 2 + 1]).then_inc(y_set, 1)
                if m % C == 0 and m + 7 < B:
                    split_ht(m + 7)
                split_next(0)
                if 1 <= m <= B:
                    act.wait_ge(kt_mm, n[m])
                    act.activation(kt[:, 0, (m - 1) % 2, :], s_ps[(m - 1) % 2][:, 0:P], ACT.Copy).then_inc(kt_hi, 1)
                if m < B - GROUP:
                    act.wait_ge(hu_mm[1], n[m + 5])
                    act.activation(hu_out(0, m + C, 1), by_graph(hu_ps[1][:, :]), ACT.Copy).then_inc(hu_hi[1], 1)
                split_next(1)
                if m < B:
                    act.wait_ge(gauss_arg, n[m + 1])
                    act.wait_ge(bias_set, n[m + 1])
                    act.activation(gauss[:, :], near[:, :], ACT.Exp, scale=inv_s2,
                                   bias=exp_bias[:, m % 2:m % 2 + 1]).then_inc(gauss_exp, 1)
                split_next(2)
                if 2 <= m <= B + 1:
                    act.wait_ge(x1_set, n[m - 1])
                    act.activation(x1[:, 0, m % 2, :], x1f[:, :], ACT.Copy).then_inc(x1_hi, 1)

            run(act, slot)

        @block.vector
        def _(dve):
            def rest(out, full, hi):
                return dve.tensor_tensor(out, full, hi.bitcast(F32), ALU.subtract)

            def split_weight(k):
                for e in range(C):
                    dve.wait_ge(w_hi, k * C + e + 1)
                    rest(w_split(1, k, e), w_raw[k][:, e, :], w_split(0, k, e)).then_inc(w_lo, 1)

            def split_product(n):
                for d in range(C):
                    dve.wait_ge(prod_hi, n * C + d + 1)
                    ps, (hi, lo), width = product_row(n, d)
                    if n < 2:
                        last = dve.scalar_tensor_tensor(lo[:, 0:P], ps[:, 0:P], 0.5, hi[:, 0:P].bitcast(F32),
                                                        ALU.mult, ALU.subtract)
                        if width > P:
                            last = rest(lo[:, P:width], ps[:, P:width], hi[:, P:width])
                    else:
                        last = rest(lo, ps, hi)
                    last.then_inc(prod_lo, 1)

            dve.memset(x1[:, 0, 0, :].bitcast(F32), 0.0).then_inc(zeros_set, 1)
            split_weight(0)
            split_weight(1)
            dve.wait_ge(adj_in, 16)
            dve.tensor_tensor(w1f[:, 0, :], adj[:, :], adj[:, :], ALU.mult).then_inc(w1_sum, 1)
            dve.wait_ge(w1_sum, 1)
            dve.wait_ge(ident_set, 3)
            dve.tensor_tensor(w1f[:, 1, :], w1f[:, 0, :], ident[:, :], ALU.add).then_inc(w1_sum, 1)
            split_product(0)
            split_weight(2)
            split_weight(3)
            dve.wait_ge(w1_hi, 1)
            rest(w1[:, 1, :], w1f[:, 1, :], w1[:, 0, :]).then_inc(w1_lo, 1)
            dve.wait_ge(gate_exp, 2)
            dve.tensor_scalar(one_e, e_gate, 1.0, None, ALU.add).then_inc(gate_ops, 1)
            dve.tensor_tensor(sig_sq[:, :], sigma, sigma, ALU.mult).then_inc(gate_ops, 1)
            dve.wait_ge(gate_ops, 2)
            dve.reciprocal(w_l, one_e).then_inc(gate_ops, 1)
            dve.reciprocal(inv_s2, sig_sq[:, :]).then_inc(gate_ops, 1)
            dve.wait_ge(gate_ops, 4)
            for k in range(2):
                dve.tensor_scalar(share[:, k, 1:2], w_l, -1.0, 1.0, ALU.mult, ALU.add).then_inc(gate_ops, 1)
            split_product(1)
            split_product(2)
            for m in range(C):
                for k in range(2):
                    dve.wait_ge(hu_hi[k], m + 1)
                    rest(hu_out(1, m, k), by_graph(early_bank(m, k)[:, :]), hu_out(0, m, k)).then_inc(hu_lo[k], 1)
            dve.wait_ge(mask_set, 1)

            def slot(m, t, n):
                q = (m - 1) % 2
                s = s_ps[m % 2]
                if m < B:
                    dve.wait_ge(p_out, n[m + 1])
                    dve.tensor_tensor_reduce(scores[:, :], p_sb[:, m % 2, 0:P], ident[:, :], 1.0, 0.0,
                                             ALU.mult, ALU.add, half_sq[:, m % 2:m % 2 + 1])
                    dve.tensor_tensor_reduce(near[:, :], p_sb[:, m % 2, P:2 * P], ident[:, :], -1.0, 0.0,
                                             ALU.mult, ALU.add, neg_half_sq[:, m % 2:m % 2 + 1]).then_inc(diag, 1)
                if 1 <= m <= B:
                    dve.wait_ge(coef_set, n[m])
                    dve.tensor_scalar(kmix[:, :], edges[:, q, 0, :], coef[:, q, 0:1], None, ALU.mult).then_inc(mix_l, 1)
                if m < B:
                    dve.wait_ge(v_hi, n[m + 1])
                    rest(v[:, 1, m % 2, :], v_ps[:, :], v[:, 0, m % 2, :]).then_inc(v_lo, 1)
                if 1 <= m <= B:
                    dve.wait_ge(mix_l, n[m])
                    dve.scalar_tensor_tensor(kmat[:, :], edges[:, q, 1, :], coef[:, q, 1:2], kmix[:, :],
                                             ALU.mult, ALU.add).then_inc(k_set, 1)
                if 3 <= m <= B + 2:
                    dve.wait_ge(l1_mm, n[m - 2])
                    if m >= B:
                        dve.wait_ge(y_set, n[m - 4])
                    dve.tensor_tensor(res2[:, (m - 3) % 2, :], l1_ps[:, :], bias[:, :], ALU.add).then_inc(res2_set, 1)
                if 2 <= m <= B + 1:
                    dve.wait_ge(ident_set, 1)
                    dve.wait_ge(stats1, n[m - 1])
                    dve.bn_aggr(moments[:, m % 2, 0, :], stats[:, 0, :]).then_inc(moments1, 1)
                if m < B - GROUP:
                    dve.wait_ge(hu_hi[0], n[m + 5])
                    rest(hu_out(1, m + C, 0), by_graph(hu_ps[0][:, :]), hu_out(0, m + C, 0)).then_inc(hu_lo[0], 1)
                if 3 <= m <= B + 2:
                    dve.wait_ge(res2_set, n[m - 2])
                    dve.bn_stats(stats[:, 1, :], res2[:, (m - 3) % 2, :]).then_inc(stats2, 1)
                    dve.wait_ge(ident_set, 1)
                    dve.wait_ge(stats2, n[m - 2])
                    dve.bn_aggr(moments[:, m % 2, 1, :], stats[:, 1, :]).then_inc(moments2, 1)
                if m < B:
                    dve.wait_ge(turned, n[m + 1])
                    dve.wait_ge(diag, n[m + 1])
                    dve.tensor_tensor(scores[:, :], s[:, 0:P], p_sb[:, m % 2, 0:P], ALU.add).then_inc(scores_set, 1)
                    dve.tensor_tensor(edges[:, m % 2, 1, :], s[:, 2 * P:3 * P], mask[:, :], ALU.mult).then_inc(over_norm, 1)
                if 1 <= m <= B:
                    dve.wait_ge(kt_hi, n[m])
                    rest(kt[:, 1, q, :], s_ps[q][:, 0:P], kt[:, 0, q, :]).then_inc(kt_lo, 1)
                if m < B:
                    dve.wait_ge(scores_set, n[m + 1])
                    dve.wait_ge(over_norm, n[m + 1])
                    dve.scalar_tensor_tensor(edges[:, m % 2, 0, :], scores[:, 0:P], 0.0, edges[:, m % 2, 1, :],
                                             ALU.max, ALU.mult, accum_out=degree[:, m % 2, 0:1]).then_inc(edges_l, 1)
                    dve.tensor_tensor(near[:, :], s[:, P:2 * P], p_sb[:, m % 2, P:2 * P], ALU.add).then_inc(gauss_arg, 1)
                if 2 <= m <= B + 1:
                    dve.wait_ge(rstd_set, n[m - 1])
                    dve.tensor_scalar(x1f[:, :], res1[:, :], moments[:, m % 2, 0, 0:1], rstd[:, m % 2, 0:1],
                                      ALU.subtract, ALU.mult).then_inc(x1_set, 1)
                if m < B:
                    dve.wait_ge(gauss_exp, n[m + 1])
                    dve.wait_ge(edges_l, n[m + 1])
                    dve.scalar_tensor_tensor(edges[:, m % 2, 1, :], gauss[:, :], 1.0, mask[:, :],
                                             ALU.min, ALU.mult, accum_out=degree[:, m % 2, 1:2]).then_inc(edges_g, 1)
                if m < B - GROUP:
                    dve.wait_ge(hu_hi[1], n[m + 5])
                    rest(hu_out(1, m + C, 1), by_graph(hu_ps[1][:, :]), hu_out(0, m + C, 1)).then_inc(hu_lo[1], 1)
                if 1 <= m <= B:
                    dve.wait_ge(kv_mm, n[m])
                    if m >= 2:
                        dve.wait_ge(x1_set, n[m - 1])
                    if (m - 1) % GROUP == 0:
                        group = (m - 1) // GROUP
                        dve.wait_ge(xn_in[group % 2], 16 * (group // 2 + 1) + 16 * t)
                    dve.tensor_tensor(res1[:, :], kv_ps[:, :], xn[:, ((m - 1) // GROUP) % 2, (m - 1) % GROUP, :],
                                      ALU.add).then_inc(res1_set, 1)
                if 2 <= m <= B + 1:
                    dve.wait_ge(x1_hi, n[m - 1])
                    rest(x1[:, 1, m % 2, :], x1f[:, :], x1[:, 0, m % 2, :]).then_inc(x1_lo, 1)
                if 1 <= m <= B:
                    dve.wait_ge(res1_set, n[m])
                    dve.bn_stats(stats[:, 0, :], res1[:, :]).then_inc(stats1, 1)

            run(dve, slot)

        @block.gpsimd
        def _(pool):
            pool.memset(ident[:, :], 0.0).then_inc(ident_set, 1)
            pool.memset(powers[:, 0, :], -0.5).then_inc(consts_set, 1)
            pool.memset(powers[:, 1, :], -1.0).then_inc(consts_set, 1)
            pool.wait_ge(ident_set, 1)
            pool.affine_select(out=ident[:, :], in_=ident[:, :], compare_op=ALU.not_equal, fill=1.0, base=0,
                               pattern=[[-1, P]], channel_multiplier=1).then_inc(ident_set, 2)
            pool.wait_ge(adj_in, 16)
            pool.affine_select(out=mask[:, :], in_=adj[:, :], compare_op=ALU.not_equal, fill=0.0, base=0,
                               pattern=[[-1, P]], channel_multiplier=1).then_inc(mask_set, 1)

            def split_ht(m):
                raw, (hi, lo) = raw_chunk(m)
                pool.tensor_tensor(lo, raw, hi.bitcast(F32), ALU.subtract).then_inc(ht_lo, 1)

            for q in range(2 * C - 1):
                pool.wait_ge(ht_hi, q + 1)
                split_ht(q)
            pool.wait_ge(consts_set, 2)
            pool.wait_ge(gate_ops, 6)

            def slot(m, t, n):
                p = m % 2

                def split_next(c):
                    q = ht_early(m, c)
                    if q is not None:
                        pool.wait_ge(ht_hi, n[q + 1])
                        split_ht(q)

                if m % C == 1 and m + 6 < B:
                    pool.wait_ge(ht_hi, n[m + 7])
                    split_ht(m + 6)
                if m < B:
                    pool.wait_ge(ident_set, 1)
                    pool.wait_ge(diag, n[m + 1])
                    pool.tensor_scalar(sq_floor[:, p:p + 1], half_sq[:, p:p + 1], 2.0, EPS * EPS,
                                       ALU.mult, ALU.max).then_inc(floor_set, 1)
                    pool.wait_ge(floor_set, n[m + 1])
                    pool.tensor_tensor(inv_norm[:, p:p + 1], sq_floor[:, p:p + 1], powers[:, 0, 0:1],
                                       ALU.pow).then_inc(norm_set, 1)
                    pool.tensor_scalar(exp_bias[:, p:p + 1], neg_half_sq[:, p:p + 1], inv_s2, None,
                                       ALU.mult).then_inc(bias_set, 1)
                if 2 <= m <= B + 2:
                    a, b = (0 if m <= B + 1 else 1), (2 if m >= 3 else 1)
                    pool.wait_ge(ident_set, 1)
                    if m <= B + 1:
                        pool.wait_ge(moments1, n[m - 1])
                    if m >= 3:
                        pool.wait_ge(moments2, n[m - 2])
                    pool.tensor_scalar(var_eps[:, p, a:b], moments[:, p, a:b, 1], LN_EPS, None, ALU.add).then_inc(var_set, 1)
                    pool.wait_ge(var_set, n[m - 1])
                    pool.tensor_tensor(rstd[:, p, a:b], var_eps[:, p, a:b], powers[:, 0, a:b], ALU.pow).then_inc(rstd_set, 1)
                split_next(0)
                split_next(1)
                if m < B:
                    pool.wait_ge(ident_set, 1)
                    pool.wait_ge(edges_l, n[m + 1])
                    pool.tensor_scalar(floored[:, p, 0:1], degree[:, p, 0:1], inv_norm[:, p:p + 1], EPS,
                                       ALU.mult, ALU.max)
                    pool.wait_ge(ident_set, 1)
                    pool.wait_ge(edges_g, n[m + 1])
                    pool.tensor_scalar(floored[:, p, 1:2], degree[:, p, 1:2], EPS, None, ALU.max).then_inc(deg_floor, 1)
                    pool.wait_ge(ident_set, 1)
                    pool.wait_ge(norm_set, n[m + 1])
                    pool.tensor_scalar(share[:, p, 0:1], inv_norm[:, p:p + 1], w_l, None, ALU.mult).then_inc(share_set, 1)
                split_next(2)
                if m < B:
                    pool.wait_ge(deg_floor, n[m + 1])
                    pool.tensor_tensor(recip[:, p, :], floored[:, p, :], powers[:, 1, :], ALU.pow).then_inc(deg_recip, 1)
                    pool.wait_ge(deg_recip, n[m + 1])
                    pool.wait_ge(share_set, n[m + 1])
                    pool.tensor_tensor(coef[:, p, :], recip[:, p, :], share[:, p, :], ALU.mult).then_inc(coef_set, 1)
                if 3 <= m <= B + 2:
                    pool.wait_ge(ident_set, 1)
                    pool.wait_ge(rstd_set, n[m - 1])
                    pool.tensor_scalar(shift[:, p:p + 1], moments[:, p, 1, 0:1], -1.0, rstd[:, p, 1:2],
                                       ALU.mult, ALU.mult).then_inc(shift_set, 1)

            run(pool, slot)


def kernel(x, adj, L0_gnn_W_lang, L0_gnn_W_grav, L0_gnn_W_V, L0_gnn_W_O, L0_gnn_gate_logit, L0_gnn_log_sigma,
           L1_gnn_bias):
    import numpy as np
    import concourse.bacc as bacc
    from concourse.bass_utils import run_bass_kernel_spmd

    x = np.asarray(x)
    batch, nodes, dim = x.shape
    xt = x.reshape(batch // GROUP, GROUP, nodes, dim // P, P).transpose(0, 4, 3, 1, 2)
    arrays = {
        "xt_dram": np.ascontiguousarray(xt).reshape(batch // GROUP, P, dim // P, GROUP * nodes),
        "x_dram": np.ascontiguousarray(x),
        "adj_dram": np.ascontiguousarray(adj),
        "w_lang_dram": np.ascontiguousarray(L0_gnn_W_lang),
        "w_grav_dram": np.ascontiguousarray(L0_gnn_W_grav),
        "w_v_dram": np.ascontiguousarray(L0_gnn_W_V),
        "w_ot_dram": np.ascontiguousarray(np.asarray(L0_gnn_W_O).T),
        "gate_dram": np.asarray(L0_gnn_gate_logit).reshape(1),
        "sigma_dram": np.asarray(L0_gnn_log_sigma).reshape(1),
        "bias_dram": np.ascontiguousarray(L1_gnn_bias),
    }
    nc = bacc.Bacc("TRN2", target_bir_lowering=False, num_devices=1)
    ins = [nc.dram_tensor(name, a.shape, mybir.dt.from_np(a.dtype), kind="ExternalInput").ap()
           for name, a in arrays.items()]
    out = nc.dram_tensor("out_dram", x.shape, mybir.dt.from_np(x.dtype), kind="ExternalOutput").ap()
    build(nc, *ins, out)
    result = run_bass_kernel_spmd(nc, [arrays], core_ids=[0])
    return result.results[0]["out_dram"]
```
